# Optimizing a Trainium2 kernel written in Bass

```python
import numpy as np
import jax
import jax.numpy as jnp

def _softmax(x, axis=-1):
    return jax.nn.softmax(x, axis=axis)

def _gelu(x):
    return jax.nn.gelu(x, approximate=True)

def _silu(x):
    return jax.nn.silu(x)

def _sigmoid(x):
    return jax.nn.sigmoid(x)

def _layernorm(x, axis=-1, eps=1e-05):
    m = jnp.mean(x, axis=axis, keepdims=True)
    v = jnp.var(x, axis=axis, keepdims=True)
    return (x - m) / jnp.sqrt(v + eps)

def _scatter_add(tgt, idx, src, axis=0):
    return tgt.at[idx].add(src)

def _segment_sum(src, seg, n):
    return jax.ops.segment_sum(src, seg, n)
kernel_name = 'mk_xattn_seq_d2_seqx_r4_d86a6b'

def setup_inputs(seed: int=0):
    np.random.seed(seed)
    _w = jnp.asarray

    def _rec_inputs():
        import jax
        import jax.numpy as jnp
        _rk = jax.random.key(seed)
        x = -0.0003929 + 0.9999 * jax.random.normal(jax.random.fold_in(_rk, 1), (16, 512, 256), jnp.float32)
        _lenS = 512 - jax.random.randint(jax.random.fold_in(_rk, 7), (16,), 0, max(1, 512 // 4) + 1, jnp.int32)
        _lenS2 = 64 - jax.random.randint(jax.random.fold_in(_rk, 8), (16,), 0, max(1, 64 // 4) + 1, jnp.int32)
        _ctx_1024P = jax.random.normal(jax.random.fold_in(_rk, 11), (16, 16, 256), jnp.float32)
        _ctx_1024c = jax.random.dirichlet(jax.random.fold_in(_rk, 511), 0.3 * jnp.ones((16,), jnp.float32), (16, 64))
        _ctx_1024t = jnp.einsum('bsk,bkd->bsd', _ctx_1024c, _ctx_1024P)
        _ctx_1024t = _ctx_1024t * jax.lax.rsqrt(jnp.mean(jnp.square(_ctx_1024t)) + 1e-12) * 0.953939
        ctx_1024 = 0.000227908 + 0.99994 * (_ctx_1024t + 0.3 * jax.random.normal(jax.random.fold_in(_rk, 611), (16, 64, 256), jnp.float32))
        itok_BxS_0_255 = jax.random.randint(jax.random.fold_in(_rk, 12), (16, 512), 0, 64, jnp.int32)
        return (x, ctx_1024, itok_BxS_0_255)
    x, ctx_1024, itok_BxS_0_255 = _rec_inputs()

    def _L0_xattn_setup():
        import jax, jax.numpy as jnp
        import numpy as np
        import math
        EPS_RMS = 1.1920929e-07
        EPS_DEN = 1e-06

        def rmsnorm(x, gamma):
            ms = jnp.mean(x * x, axis=-1, keepdims=True)
            return x * jax.lax.rsqrt(ms + EPS_RMS) * gamma
        key = jax.random.key(seed)
        ks = jax.random.split(key, 8)
        B, T, K, D = (4, 1024, 64, 256)
        x_tokens = jax.random.normal(ks[0], (B, T, D), dtype=jnp.float32)
        ctx = jax.random.normal(ks[1], (B, K, D), dtype=jnp.float32)
        idx = jnp.sort(jax.random.randint(ks[2], (B, T), 0, K), axis=-1)
        s = 1.0 / math.sqrt(D)
        Wq = jax.random.normal(ks[3], (D, D), dtype=jnp.float32) * s
        Wk = jax.random.normal(ks[4], (D, D), dtype=jnp.float32) * s
        Wv = jax.random.normal(ks[5], (D, D), dtype=jnp.float32) * s
        Wo = jax.random.normal(ks[6], (D, D), dtype=jnp.float32) * s
        return {'x_tokens': x_tokens, 'ctx': ctx, 'ctx_index_per_token': idx, 'gamma_q': jnp.ones((D,), jnp.float32), 'gamma_kv': jnp.ones((D,), jnp.float32), 'Wq': Wq, 'Wk': Wk, 'Wv': Wv, 'Wo': Wo}
    _L0_xattn_all = _L0_xattn_setup()
    _L0_xattn_in = {k: v for k, v in _L0_xattn_all.items() if k in ('gamma_q', 'gamma_kv', 'Wq', 'Wk', 'Wv', 'Wo')}
    del _L0_xattn_all

    def _L1_xattn_setup():
        import jax, jax.numpy as jnp
        import numpy as np
        D_MODEL = 256
        PROJ = 256
        LN_EPS = 1e-05
        key = jax.random.key(seed)
        ks = jax.random.split(key, 12)
        B, Q, N = (16, 16, 1024)
        s = 1.0 / np.sqrt(D_MODEL)
        sp = 1.0 / np.sqrt(PROJ)
        return {'virtual_node': jax.random.normal(ks[0], (B, Q, D_MODEL), jnp.float32), 'node_features': jax.random.normal(ks[1], (B, N, D_MODEL), jnp.float32), 'Wq': jax.random.uniform(ks[2], (D_MODEL, PROJ), jnp.float32, -s, s), 'bq': jax.random.uniform(ks[3], (PROJ,), jnp.float32, -s, s), 'Wk': jax.random.uniform(ks[4], (D_MODEL, PROJ), jnp.float32, -s, s), 'bk': jax.random.uniform(ks[5], (PROJ,), jnp.float32, -s, s), 'Wv': jax.random.uniform(ks[6], (D_MODEL, PROJ), jnp.float32, -s, s), 'bv': jax.random.uniform(ks[7], (PROJ,), jnp.float32, -s, s), 'Wf': jax.random.uniform(ks[8], (PROJ, D_MODEL), jnp.float32, -sp, sp), 'bf': jax.random.uniform(ks[9], (D_MODEL,), jnp.float32, -sp, sp), 'ln_gamma': jnp.ones((D_MODEL,), jnp.float32), 'ln_beta': jnp.zeros((D_MODEL,), jnp.float32)}
    _L1_xattn_all = _L1_xattn_setup()
    _L1_xattn_in = {k: v for k, v in _L1_xattn_all.items() if k in ('Wq', 'bq', 'Wk', 'bk', 'Wv', 'bv', 'Wf', 'bf', 'ln_gamma', 'ln_beta')}
    del _L1_xattn_all
    return {'x': x, 'ctx_1024': ctx_1024, 'itok_BxS_0_255': itok_BxS_0_255, 'L0_xattn_gamma_q': _L0_xattn_in['gamma_q'], 'L0_xattn_gamma_kv': _L0_xattn_in['gamma_kv'], 'L0_xattn_Wq': _L0_xattn_in['Wq'], 'L0_xattn_Wk': _L0_xattn_in['Wk'], 'L0_xattn_Wv': _L0_xattn_in['Wv'], 'L0_xattn_Wo': _L0_xattn_in['Wo'], 'L1_xattn_Wq': _L1_xattn_in['Wq'], 'L1_xattn_bq': _L1_xattn_in['bq'], 'L1_xattn_Wk': _L1_xattn_in['Wk'], 'L1_xattn_bk': _L1_xattn_in['bk'], 'L1_xattn_Wv': _L1_xattn_in['Wv'], 'L1_xattn_bv': _L1_xattn_in['bv'], 'L1_xattn_Wf': _L1_xattn_in['Wf'], 'L1_xattn_bf': _L1_xattn_in['bf'], 'L1_xattn_ln_gamma': _L1_xattn_in['ln_gamma'], 'L1_xattn_ln_beta': _L1_xattn_in['ln_beta']}

def reference(x, ctx_1024, itok_BxS_0_255, L0_xattn_gamma_q, L0_xattn_gamma_kv, L0_xattn_Wq, L0_xattn_Wk, L0_xattn_Wv, L0_xattn_Wo, L1_xattn_Wq, L1_xattn_bq, L1_xattn_Wk, L1_xattn_bk, L1_xattn_Wv, L1_xattn_bv, L1_xattn_Wf, L1_xattn_bf, L1_xattn_ln_gamma, L1_xattn_ln_beta):
    import jax
    import jax.numpy as jnp

    def _L0_xattn_ref(x_tokens, ctx, ctx_index_per_token, gamma_q, gamma_kv, Wq, Wk, Wv, Wo):
        import jax, jax.numpy as jnp
        import numpy as np
        import math
        EPS_RMS = 1.1920929e-07
        EPS_DEN = 1e-06

        def rmsnorm(x, gamma):
            ms = jnp.mean(x * x, axis=-1, keepdims=True)
            return x * jax.lax.rsqrt(ms + EPS_RMS) * gamma
        B, T, D = x_tokens.shape
        K = ctx.shape[1]
        H = 16
        hd = D // H

        def split(x):
            return x.reshape(B, -1, H, hd).transpose(0, 2, 1, 3)
        q = split(rmsnorm(x_tokens, gamma_q) @ Wq.T)
        kn = rmsnorm(ctx, gamma_kv)
        k = split(kn @ Wk.T)
        v = split(kn @ Wv.T)
        ctx_pos = jnp.arange(K)[None, None, :]
        mask = (jnp.abs(ctx_pos - ctx_index_per_token[:, :, None]) <= 1)[:, None]
        scores = jnp.einsum('bhqd,bhkd->bhqk', q, k) / math.sqrt(hd)
        w = jnp.square(jax.nn.relu(scores))
        w = jnp.where(mask, w, 0.0)
        denom = jnp.maximum(w.sum(-1, keepdims=True), EPS_DEN)
        out = jnp.einsum('bhqk,bhkd->bhqd', w / denom, v)
        out = out.transpose(0, 2, 1, 3).reshape(B, T, D)
        return x_tokens + out @ Wo.T

    def _L1_xattn_ref(virtual_node, node_features, Wq, bq, Wk, bk, Wv, bv, Wf, bf, ln_gamma, ln_beta):
        import jax, jax.numpy as jnp
        import numpy as np
        D_MODEL = 256
        PROJ = 256
        LN_EPS = 1e-05
        gelu = lambda x: jax.nn.gelu(x, approximate=False)
        q = gelu(jnp.einsum('bqd,dp->bqp', virtual_node, Wq) + bq)
        k = gelu(jnp.einsum('bnd,dp->bnp', node_features, Wk) + bk)
        v = gelu(jnp.einsum('bnd,dp->bnp', node_features, Wv) + bv)
        scores = jnp.einsum('bqp,bnp->bqn', q, k)
        w = jax.nn.softmax(scores, axis=-1)
        attended = jnp.einsum('bqn,bnp->bqp', w, v)
        out = jnp.einsum('bqp,pd->bqd', attended, Wf) + bf
        x = out + virtual_node
        mu = jnp.mean(x, axis=-1, keepdims=True)
        var = jnp.mean(jnp.square(x - mu), axis=-1, keepdims=True)
        return (x - mu) * jax.lax.rsqrt(var + LN_EPS) * ln_gamma + ln_beta
    x = _L0_xattn_ref(x, ctx_1024, itok_BxS_0_255, L0_xattn_gamma_q, L0_xattn_gamma_kv, L0_xattn_Wq, L0_xattn_Wk, L0_xattn_Wv, L0_xattn_Wo)
    x = _L1_xattn_ref(x, ctx_1024, L1_xattn_Wq, L1_xattn_bq, L1_xattn_Wk, L1_xattn_bk, L1_xattn_Wv, L1_xattn_bv, L1_xattn_Wf, L1_xattn_bf, L1_xattn_ln_gamma, L1_xattn_ln_beta)
    return x

_drawn_inputs = setup_inputs


def setup_inputs(seed=0):
    import zlib

    import numpy as np

    out = dict(_drawn_inputs(seed))
    spreads = {'L0_xattn_gamma_q': (1.0, 0.2),
     'L0_xattn_gamma_kv': (1.0, 0.2),
     'L1_xattn_ln_gamma': (1.0, 0.2),
     'L1_xattn_ln_beta': (0.0, 0.1)}
    factors = {'L1_xattn_bq': 8.0, 'L1_xattn_bk': 8.0, 'L1_xattn_bv': 6.521}
    for name, (base, spread) in spreads.items():
        noise = np.random.default_rng([zlib.crc32(name.encode()), seed]).standard_normal(out[name].shape)
        drawn = base * np.exp(spread * noise) if base else spread * noise
        out[name] = jnp.asarray(drawn.astype(out[name].dtype))
    for name, factor in factors.items():
        out[name] = (out[name] * factor).astype(out[name].dtype)
    return out
```

```python
import concourse.bass as bass
from concourse import mybir
from contextlib import ExitStack

B, T, D, K, H = 16, 512, 256, 64, 16
HD = D // H
P = 128
DC = D // P
TT = T // P
PAIRS = H // 2
HPH = H // DC
EPS_RMS = 1.1920929e-07
EPS_DEN = 1e-06
LN_EPS = 1e-05
CT = B * K // P

C_ID, C_HEAD, C_HALF, C_DEN, C_POS, C_END = 0, 128, 136, 138, 234, 236


def xattn_pair(nc: bass.Bass, xT, ctx, ctxT, idx, gq, gkv, wq0T, wk0T, wv0T, wo0T,
               wq1, bq1, wk1, bk1, wv1, bv1, wf1, bf1, ln_g, ln_b, consts, out):
    f32 = mybir.dt.float32
    i32 = mybir.dt.int32
    ALU = mybir.AluOpType
    ACT = mybir.ActivationFunctionType
    AX = mybir.AxisListType

    es = ExitStack()
    with es:
        def sb(name, shape, dt=f32):
            return es.enter_context(nc.sbuf_tensor(name, shape, dt))

        def sem(name):
            return es.enter_context(nc.semaphore(name))

        cst = sb("cst", [P, C_END])
        ident = cst[:, C_ID:C_ID + P]
        head_mask = cst[:, C_HEAD:C_HEAD + HPH]
        half_mask = cst[:, C_HALF:C_HALF + 2]
        den_sel = cst[:, C_DEN:C_DEN + 96].rearrange("p (s c) -> p s c", s=3)
        pos = cst[:, C_POS:C_POS + 1]
        pos1 = cst[:, C_POS + 1:C_POS + 2]
        wts = {n: sb("w_" + n, [P, DC, D]) for n in ("q0", "o0", "q1")}
        vec = sb("vec", [P, 5, DC])
        bf_row = sb("bf_row", [P, D])
        lng_row = sb("lng_row", [P, D])
        lnb_row = sb("lnb_row", [P, D])
        minus_half = sb("minus_half", [P, CT])
        ln_eps = sb("ln_eps", [P, TT])
        xT_all = sb("xT_all", [P, B, DC, T])
        k0T = sb("k0T", [P, DC, B * K])
        v0d = sb("v0d", [P, B, D])
        k1T = sb("k1T", [P, DC, B * K + K])
        vfd = sb("vfd", [P, B, D])

        kblk = sb("kblk", [P, DC, HPH * K])
        vblk = sb("vblk", [P, PAIRS, 2 * HD])
        vf = sb("vf", [P, D])
        idx_sb = sb("idx_sb", [P, T], i32)
        above = sb("above", [P, T])
        mask = sb("mask", [P, T])
        q0T = sb("q0T", [P, DC, T])
        xsq = sb("xsq", [P, DC, T])
        w = sb("w", [P, PAIRS, T])
        den_sb = sb("den_sb", [P, T])
        dmin = sb("dmin", [P, TT])
        dcl = sb("dcl", [P, TT, H])
        rden = sb("rden", [P, TT, H])
        rexp = sb("rexp", [P, TT, D])
        rep_sb = sb("rep_sb", [P, DC, T])
        oT_xpT = sb("oT_xpT", [P, 2, DC, T])
        oT, xpT = oT_xpT[:, 0, :, :], oT_xpT[:, 1, :, :]
        q1T_zT = sb("q1T_zT", [P, 2, DC, T])
        q1T, zT = q1T_zT[:, 0, :, :], q1T_zT[:, 1, :, :]
        smax = sb("smax", [P, TT])
        sdiff = sb("sdiff", [P, TT, K])
        ex = sb("ex", [P, TT, K])
        ssum = sb("ssum", [P, TT])
        rsum = sb("rsum", [P, TT])
        en = sb("en", [P, TT, 2 * K])
        eT = sb("eT", [P, T])
        stats = sb("stats", [P, TT, 6])
        mean_gap, nmean2, m2_sum, gap_sq, var = (sb(n, [P, TT]) for n in ("mean_gap", "nmean2", "m2_sum", "gap_sq", "var"))
        veps = sb("veps", [P, TT])
        rstd = sb("rstd", [P, TT])
        nmean = sb("nmean", [P, TT])
        nbias = sb("nbias", [P, TT])
        zn_zo = sb("zn_zo", [P, 2, TT, D])
        zn, zo = zn_zo[:, 0, :, :], zn_zo[:, 1, :, :]

        ctx_sb = w[:, 0:4, :].rearrange("p a b -> p (a b)").rearrange("p (t d) -> p t d", d=D)
        kn = w[:, 4:8, :].rearrange("p a b -> p (a b)").rearrange("p (t d) -> p t d", d=D)
        ctxT_sb = q1T_zT[:, :, :, :].rearrange("p a b c -> p a (b c)")
        for n, name in enumerate(("k0", "v0", "k1", "v1")):
            wts[name] = xT_all[:, B // 2 - 2 + n // 2, n % 2, :].rearrange("p (c d) -> p c d", c=DC)
        wts["f1"] = xT_all[:, B // 2 - 3, 0, :].rearrange("p (c d) -> p c d", c=DC)
        knT = xT_all[:, B // 2:B // 2 + 4, :, :].rearrange("p a b c -> p (a b c)").rearrange("p (c b j k) -> p c b j k", c=DC, j=2, k=K)
        v1T = xT_all[:, B // 2 + 4:, :, :].rearrange("p a b c -> p (a b c)").rearrange("p (c b j k) -> p c b j k", c=DC, j=2, k=K)
        csq = xsq[:, 0, 0:D]
        cms = sb("cms", [P, CT])
        cmean = sb("cmean", [P, CT])
        crs = sb("crs", [P, CT])

        ps = es.enter_context(nc.psum_tensor("ps", [P, 8, 512], f32))

        consts_in, ctx_in, w0_in, w1_in, x_in, idx_in = map(sem, (
            "consts_in", "ctx_in", "w0_in", "w1_in", "x_in", "idx_in"))
        folded, cms_done, cmean_done, crs_done, kn_done, knT_mm, knT_cp, ev_mm, ev_cp, half_set = map(sem, (
            "folded", "cms_done", "cmean_done", "crs_done", "kn_done", "knT_mm", "knT_cp", "ev_mm", "ev_cp",
            "half_set"))
        en_zero = sem("en_zero")
        kblk_ready, vblk_ready, vf_ready = map(sem, ("kblk_ready", "vblk_ready", "vf_ready"))
        above_ready, mask_ready, xsq_ready = map(sem, ("above_ready", "mask_ready", "xsq_ready"))
        q0_mm, q0_ready, s_mm, relu_done, w_ready = map(sem, ("q0_mm", "q0_ready", "s_mm", "relu_done", "w_ready"))
        den_mm, num_mm, den_cp, denT_mm, dmin_ready, dcl_ready, rden_ready = map(sem, (
            "den_mm", "num_mm", "den_cp", "denT_mm", "dmin_ready", "dcl_ready", "rden_ready"))
        rexp_ready, rep_mm, rep_cp, o_ready = map(sem, ("rexp_ready", "rep_mm", "rep_cp", "o_ready"))
        xp_mm, xp_ready, q1_mm, q1_ready, sc_mm = map(sem, ("xp_mm", "xp_ready", "q1_mm", "q1_ready", "sc_mm"))
        smax_ready, sdiff_ready, ex_ready, ssum_ready, rsum_ready, en_ready = map(sem, (
            "smax_ready", "sdiff_ready", "ex_ready", "ssum_ready", "rsum_ready", "en_ready"))
        eT_mm, eT_ready, att_mm, z_ready, zt_mm = map(sem, ("eT_mm", "eT_ready", "att_mm", "z_ready", "zt_mm"))
        stats_ready, parts_ready, gap_ready, var_ready, veps_ready, rstd_ready, nmean_ready, nbias_ready = map(sem, (
            "stats_ready", "parts_ready", "gap_ready", "var_ready", "veps_ready", "rstd_ready", "nmean_ready", "nbias_ready"))
        zn_ready, zg_ready, zo_ready, out_done = map(sem, ("zn_ready", "zg_ready", "zo_ready", "out_done"))

        block = es.enter_context(nc.Block())

        FIRST_STEADY, LAST_STEADY = 2, B - 1

        def steps(engine, step):
            step(0, None)
            step(1, 0)
            with engine.Fori(FIRST_STEADY, LAST_STEADY) as i:
                step(i, i - 1)
            step(B - 1, B - 2, last=True)
            step(None, B - 1)

        def after(n):
            return n + 1

        @block.sync
        def _(sp):
            sp.dma_start(cst[:, :], consts).then_inc(consts_in, 16)
            sp.dma_start(ctx_sb, ctx.rearrange("(t p) d -> p t d", p=P)).then_inc(ctx_in, 16)
            for i, v in enumerate((gq, gkv, bq1, bk1, bv1)):
                sp.dma_start(vec[:, i, :], v).then_inc(consts_in, 16)
            for n, v in (("k0", wk0T), ("v0", wv0T), ("q0", wq0T), ("o0", wo0T)):
                sp.dma_start(wts[n][:, :, :], v.rearrange("(c p) e -> p c e", p=P)).then_inc(w0_in, 16)
            sp.dma_start(ctxT_sb[:, :, :], ctxT.rearrange("(c p) n -> p c n", p=P)).then_inc(w1_in, 16)
            for n, v in (("k1", wk1), ("v1", wv1), ("f1", wf1), ("q1", wq1)):
                sp.dma_start(wts[n][:, :, :], v.rearrange("(c p) e -> p c e", p=P)).then_inc(w1_in, 16)
            for t, v in ((bf_row, bf1), (lng_row, ln_g), (lnb_row, ln_b)):
                sp.dma_start(t[:, :], v.partition_broadcast(P)).then_inc(w1_in, 16)

            def load(i):
                sp.dma_start(xT_all[:, i, :, :], xT[i].rearrange("(c p) t -> p c t", p=P)).then_inc(x_in, 16)
                sp.dma_start(idx_sb[:, :], idx[i].partition_broadcast(P)).then_inc(idx_in, 16)

            load(0)
            with sp.Fori(1, B) as i:
                sp.wait_ge(x_in, 16 * i)
                sp.wait_ge(mask_ready, i)
                load(i)

        @block.gpsimd
        def _(pool):
            nc.gpsimd.memset(minus_half[:, :], -0.5).then_inc(half_set, 1)
            nc.gpsimd.memset(ln_eps[:, :], LN_EPS).then_inc(half_set, 1)
            nc.gpsimd.memset(en[:, :, :], 0.0).then_inc(en_zero, 1)
            nc.gpsimd.memset(k1T[:, :, B * K:], 0.0).then_inc(en_zero, 1)
            pool.wait_ge(cms_done, CT)
            nc.gpsimd.tensor_scalar(cmean[:, :], cms[:, :], 1.0 / D, EPS_RMS, ALU.mult, ALU.add).then_inc(cmean_done, 1)
            pool.wait_ge(cmean_done, 1)
            pool.wait_ge(half_set, 2)
            nc.gpsimd.tensor_tensor(crs[:, :], cmean[:, :], minus_half[:, :], ALU.pow).then_inc(crs_done, 1)

            def build_kblk(f):
                for g in range(DC):
                    last = nc.gpsimd.tensor_tensor(
                        kblk[:, g, :].rearrange("p (h k) -> p h k", k=K),
                        k0T[:, g, bass.ts(f, K)].unsqueeze(1).broadcast_to([P, HPH, K]),
                        head_mask.unsqueeze(2).broadcast_to([P, HPH, K]), ALU.mult)
                last.then_inc(kblk_ready, 1)

            def build_vblk(f):
                nc.gpsimd.tensor_tensor(
                    vblk[:, :, :].rearrange("p c (j d) -> p c j d", j=2),
                    v0d[:, f, :].rearrange("p (c j d) -> p c j d", j=2, d=HD),
                    half_mask.unsqueeze(1).unsqueeze(3).broadcast_to([P, PAIRS, 2, HD]),
                    ALU.mult).then_inc(vblk_ready, 1)

            pool.wait_ge(consts_in, 16 * 6)
            pool.wait_ge(ev_cp, 4 + B)
            build_kblk(0)
            build_vblk(0)
            pool.wait_ge(ev_cp, 4 + B + 8 + B)

            def step(f, b, last=False):
                if b is not None:
                    if f is None or not (isinstance(b, int) and b == 0):
                        pool.wait_ge(att_mm, b)
                    nc.gpsimd.tensor_copy(vf[:, :], vfd[:, b, :]).then_inc(vf_ready, 1)
                if f is not None and not last:
                    pool.wait_ge(s_mm, 4 * f + 4)
                    build_kblk(f + 1)
                    pool.wait_ge(num_mm, f + 1)
                    build_vblk(f + 1)
                if b is not None:
                    pool.wait_ge(var_ready, b + 1)
                    nc.gpsimd.tensor_tensor(veps[:, :], var[:, :], ln_eps[:, :], ALU.add).then_inc(veps_ready, 1)
                    pool.wait_ge(veps_ready, b + 1)
                    nc.gpsimd.tensor_tensor(rstd[:, :], veps[:, :], minus_half[:, 0:TT], ALU.pow).then_inc(rstd_ready, 1)
                    pool.wait_ge(rstd_ready, b + 1)
                    pool.wait_ge(nmean_ready, b + 1)
                    nc.gpsimd.tensor_tensor(nbias[:, :], nmean[:, :], rstd[:, :], ALU.mult).then_inc(nbias_ready, 1)
                    pool.wait_ge(zn_ready, b + 1)
                    if not (isinstance(b, int) and b == 0):
                        pool.wait_ge(out_done, 16 * b)
                    nc.gpsimd.tensor_tensor(zo[:, :, :], zn[:, :, :],
                                            lng_row[:, :].unsqueeze(1).broadcast_to([P, TT, D]), ALU.mult).then_inc(zg_ready, 1)
                    pool.wait_ge(zg_ready, b + 1)
                    nc.gpsimd.tensor_tensor(zo[:, :, :], zo[:, :, :],
                                            lnb_row[:, :].unsqueeze(1).broadcast_to([P, TT, D]), ALU.add).then_inc(zo_ready, 1)
                    pool.wait_ge(zo_ready, b + 1)
                    pool.dma_start(out[b].rearrange("(j p) d -> p j d", p=P), zo[:, :, :]).then_inc(out_done, 16)

            steps(pool, step)
            pool.wait_ge(out_done, 16 * B)

        @block.tensor
        def _(pe):
            mm = nc.tensor.matmul

            pe.wait_ge(consts_in, 16 * 6)
            for t in range(CT):
                pe.wait_ge(kn_done, t + 1)
                for c in range(DC):
                    if t >= 4 and c == 0:
                        pe.wait_ge(knT_cp, t - 3)
                    last = nc.tensor.transpose(ps[:, t % 4, c * P:(c + 1) * P], kn[:, t, c * P:(c + 1) * P], ident)
                last.then_inc(knT_mm, 1)
            evac = 0

            def bank():
                if evac >= 4:
                    pe.wait_ge(ev_cp, evac - 3)
                return ps[:, 4 + evac % 4, :]

            pe.wait_ge(knT_cp, CT)
            pe.wait_ge(folded, 3)
            pe.wait_ge(w0_in, 16 * 4)
            for e in range(DC):
                for n in range(2):
                    o = bank()
                    for c in range(DC):
                        last = mm(o, wts["k0"][:, c, e * P:(e + 1) * P], knT[:, c, n * 8:(n + 1) * 8, 0, :],
                                  start=(c == 0), stop=(c == DC - 1))
                    last.then_inc(ev_mm, 1)
                    evac += 1
            for i in range(B):
                o = bank()[:, 0:D]
                for c in range(DC):
                    last = mm(o, knT[:, c, i, :, :].rearrange("p j k -> p (j k)"), wts["v0"][:, c, :],
                              start=(c == 0), stop=(c == DC - 1))
                last.then_inc(ev_mm, 1)
                evac += 1
            pe.wait_ge(w1_in, 16 * 8)
            for name in ("k1", "v1"):
                for e in range(DC):
                    for n in range(2):
                        o = bank()
                        for c in range(DC):
                            last = mm(o, wts[name][:, c, e * P:(e + 1) * P], ctxT_sb[:, c, n * 512:(n + 1) * 512],
                                      start=(c == 0), stop=(c == DC - 1))
                        last.then_inc(ev_mm, 1)
                        evac += 1
            pe.wait_ge(ev_cp, evac)
            for i in range(B):
                o = bank()[:, 0:D]
                for c in range(DC):
                    last = mm(o, v1T[:, c, i, :, :].rearrange("p j k -> p (j k)"), wts["f1"][:, c, :],
                              start=(c == 0), stop=(c == DC - 1))
                last.then_inc(ev_mm, 1)
                evac += 1
            pe.wait_ge(ev_cp, evac)

            def project(bank0, weights, moving, done):
                for e in range(DC):
                    for c in range(DC):
                        last = mm(ps[:, bank0 + e, :], weights[:, c, e * P:(e + 1) * P], moving(c),
                                  start=(c == 0), stop=(c == DC - 1))
                last.then_inc(done, 1)

            def scores(f, b, pairs):
                for c in pairs:
                    if c == 2 and b is not None:
                        pe.wait_ge(xp_ready, b + 1)
                    if c >= 4 and c % 2 == 0:
                        pe.wait_ge(relu_done, 4 * f + (c - 4) // 2 + 1)
                    g, h = c // 4, c % 4
                    last = mm(ps[:, c % 4, :], kblk[:, g, h * P:(h + 1) * P], q0T[:, g, :], start=True, stop=True)
                    if c % 2:
                        last.then_inc(s_mm, 1)

            def step(f, b, last=False):
                steady = not isinstance(f if f is not None else b, int)
                if f is not None:
                    pe.wait_ge(x_in, 16 * f + 16)
                    if not (isinstance(f, int) and f < 2):
                        pe.wait_ge(z_ready, f - 1)
                    project(0, wts["q0"], lambda c: xT_all[:, f, c, :], q0_mm)
                if b is not None:
                    pe.wait_ge(o_ready, b + 1)
                    project(2, wts["o0"], lambda c: oT[:, c, :], xp_mm)
                if f is not None:
                    pe.wait_ge(q0_ready, f + 1)
                    pe.wait_ge(kblk_ready, f + 1)
                    scores(f, b, range(0, 4))
                if b is not None:
                    pe.wait_ge(xp_ready, b + 1)
                    if not (isinstance(b, int) and b < 1):
                        pe.wait_ge(zn_ready, b)
                    project(6, wts["q1"], lambda c: xpT[:, c, :], q1_mm)
                if f is not None:
                    scores(f, b, range(4, PAIRS))
                if b is not None:
                    pe.wait_ge(q1_ready, b + 1)
                    for j in range(TT):
                        for c in range(DC):
                            mmi = mm(ps[:, 7, j * P:(j + 1) * P], q1T[:, c, j * P:(j + 1) * P],
                                     k1T[:, c, bass.ds(b * K, 2 * K)], start=(c == 0), stop=(c == DC - 1))
                    mmi.then_inc(sc_mm, 1)
                if f is not None:
                    pe.wait_ge(xsq_ready, f + 1)
                    pe.wait_ge(vblk_ready, f + 1)
                    for g in range(DC):
                        pe.wait_ge(w_ready, 4 * f + 2 * g + 2)
                        for q in range(4):
                            mmi = mm(ps[32 * q:32 * q + 32, 6, :], den_sel[:, g, :], w[:, 4 * g + q, :],
                                     start=(g == 0), stop=(g == DC - 1 and q > 0))
                        if g == DC - 1:
                            for c in range(DC):
                                mmi = mm(ps[0:32, 6, :], den_sel[:, 2, :], xsq[:, c, :], start=False, stop=(c == DC - 1))
                            mmi.then_inc(den_mm, 1)
                        for q in range(4):
                            mmi = mm(ps[32 * q:32 * q + 32, 4 + g, :], vblk[:, 4 * g + q, :], w[:, 4 * g + q, :],
                                     start=True, stop=True)
                    mmi.then_inc(num_mm, 1)
                if b is not None:
                    pe.wait_ge(en_ready, b + 1)
                    for j in range(TT):
                        mmi = nc.tensor.transpose(ps[:, 7, j * P:(j + 1) * P], en[:, j, :], ident)
                    mmi.then_inc(eT_mm, 1)
                if f is not None:
                    pe.wait_ge(den_cp, f + 1)
                    for j in range(TT):
                        mmi = nc.tensor.transpose(ps[:, 6, j * P:(j + 1) * P], den_sb[:, j * P:(j + 1) * P], ident)
                    mmi.then_inc(denT_mm, 1)
                if b is not None:
                    pe.wait_ge(eT_ready, b + 1)
                    pe.wait_ge(vf_ready, b + 1)
                    for e in range(DC):
                        mmi = mm(ps[:, e, :], vf[:, e * P:(e + 1) * P], eT[:, :], start=True, stop=True)
                    mmi.then_inc(att_mm, 1)
                if f is not None:
                    pe.wait_ge(rexp_ready, f + 1)
                    for g in range(DC):
                        for j in range(TT):
                            mmi = nc.tensor.transpose(
                                ps[:, 2 + g, j * P:(j + 1) * P],
                                rexp[:, j, g * P:(g + 1) * P], ident)
                    mmi.then_inc(rep_mm, 1)
                if b is not None:
                    pe.wait_ge(z_ready, b + 1)
                    for j in range(TT):
                        for c in range(DC):
                            mmi = nc.tensor.transpose(ps[:, 6 + j // 2, (j % 2) * D + c * P:(j % 2) * D + (c + 1) * P],
                                                      zT[:, c, j * P:(j + 1) * P], ident)
                    mmi.then_inc(zt_mm, 1)

            steps(pe, step)

        @block.scalar
        def _(act):
            act.wait_ge(ctx_in, 16)
            for t in range(CT):
                if t:
                    act.wait_ge(cms_done, t)
                nc.scalar.activation(csq, ctx_sb[:, t, :], ACT.Square, accum_out=cms[:, t:t + 1]).then_inc(cms_done, 1)
            for t in range(CT):
                act.wait_ge(knT_mm, t + 1)
                for c in range(DC):
                    last = nc.scalar.activation(
                        knT[:, c, 2 * t:2 * t + 2, :, :],
                        ps[:, t % 4, c * P:(c + 1) * P].rearrange("p (b k) -> p b k", k=K).unsqueeze(2).broadcast_to([P, 2, 2, K]),
                        ACT.Copy)
                last.then_inc(knT_cp, 1)
            n = 0
            for e in range(DC):
                for h in range(2):
                    act.wait_ge(ev_mm, n + 1)
                    nc.scalar.activation(k0T[:, e, h * 512:(h + 1) * 512], ps[:, 4 + n % 4, :], ACT.Copy).then_inc(ev_cp, 1)
                    n += 1
            for i in range(B):
                act.wait_ge(ev_mm, n + 1)
                nc.scalar.activation(v0d[:, i, :], ps[:, 4 + n % 4, 0:D], ACT.Copy).then_inc(ev_cp, 1)
                n += 1
            for e in range(DC):
                for h in range(2):
                    act.wait_ge(ev_mm, n + 1)
                    nc.scalar.activation(k1T[:, e, h * 512:(h + 1) * 512], ps[:, 4 + n % 4, :], ACT.Gelu,
                                         bias=vec[:, 3, e:e + 1]).then_inc(ev_cp, 1)
                    n += 1
            for e in range(DC):
                for h in range(2):
                    act.wait_ge(ev_mm, n + 1)
                    nc.scalar.activation(
                        v1T[:, e, 8 * h:8 * h + 8, :, :],
                        ps[:, 4 + n % 4, :].rearrange("p (b k) -> p b k", k=K).unsqueeze(2).broadcast_to([P, 8, 2, K]),
                        ACT.Gelu, bias=vec[:, 4, e:e + 1]).then_inc(ev_cp, 1)
                    n += 1

            def square(f, k):
                act.wait_ge(relu_done, 4 * f + k + 1)
                nc.scalar.activation(w[:, 2 * k:2 * k + 2, :], w[:, 2 * k:2 * k + 2, :], ACT.Square).then_inc(w_ready, 1)

            def step(f, b, last=False):
                if f is not None:
                    act.wait_ge(x_in, 16 * f + 16)
                    if not (isinstance(f, int) and f == 0):
                        act.wait_ge(den_mm, f)
                    nc.scalar.activation(xsq[:, :, :], xT_all[:, f, :, :], ACT.Square).then_inc(xsq_ready, 1)
                    act.wait_ge(q0_mm, f + 1)
                    nc.scalar.activation(q0T[:, :, :], ps[:, 0:2, :], ACT.Copy).then_inc(q0_ready, 1)
                    square(f, 0)
                    square(f, 1)
                if b is not None:
                    act.wait_ge(q1_mm, b + 1)
                    for e in range(DC):
                        i = nc.scalar.activation(q1T[:, e, :], ps[:, 6 + e, :], ACT.Gelu, bias=vec[:, 2, e:e + 1])
                    i.then_inc(q1_ready, 1)
                if f is not None:
                    square(f, 2)
                    square(f, 3)
                if b is not None:
                    act.wait_ge(sdiff_ready, b + 1)
                    nc.scalar.activation(ex[:, :, :], sdiff[:, :, :], ACT.Exp).then_inc(ex_ready, 1)
                if f is not None:
                    act.wait_ge(den_mm, f + 1)
                    nc.scalar.activation(den_sb[:, :], ps[:, 6, :], ACT.Copy).then_inc(den_cp, 1)
                if b is not None:
                    act.wait_ge(eT_mm, b + 1)
                    nc.scalar.activation(eT[:, :], ps[:, 7, :], ACT.Copy).then_inc(eT_ready, 1)
                if f is not None:
                    act.wait_ge(rep_mm, f + 1)
                    nc.scalar.activation(rep_sb[:, :, :], ps[:, 2:4, :], ACT.Copy).then_inc(rep_cp, 1)
                if b is not None:
                    act.wait_ge(zt_mm, b + 1)
                    act.wait_ge(nbias_ready, b + 1)
                    if not (isinstance(b, int) and b == 0):
                        act.wait_ge(zg_ready, b)
                    for j in range(TT):
                        i = nc.scalar.activation(zn[:, j, :], ps[:, 6 + j // 2, (j % 2) * D:(j % 2 + 1) * D], ACT.Identity,
                                                 bias=nbias[:, j:j + 1], scale=rstd[:, j:j + 1])
                    i.then_inc(zn_ready, 1)

            steps(act, step)

        @block.vector
        def _(dve):
            V = nc.vector
            dve.wait_ge(consts_in, 16 * 6)
            dve.wait_ge(w0_in, 16 * 4)
            for n, g in (("k0", 1), ("v0", 1), ("q0", 0)):
                for c in range(DC):
                    last = V.tensor_scalar(wts[n][:, c, :], wts[n][:, c, :], vec[:, g, c:c + 1], None, ALU.mult)
                last.then_inc(folded, 1)
            dve.wait_ge(crs_done, 1)
            for t in range(CT):
                V.tensor_scalar(kn[:, t, :], ctx_sb[:, t, :], crs[:, t:t + 1], None, ALU.mult).then_inc(kn_done, 1)
            n = 4 + B + 8
            dve.wait_ge(w1_in, 16 * 8)
            for i in range(B):
                dve.wait_ge(ev_mm, n + 1)
                V.tensor_tensor(vfd[:, i, :], ps[:, 4 + n % 4, 0:D], bf_row[:, :], ALU.add).then_inc(ev_cp, 1)
                n += 1
            dve.wait_ge(en_zero, 2)

            def relu_mask(f, k):
                dve.wait_ge(s_mm, 4 * f + k + 1)
                V.scalar_tensor_tensor(w[:, 2 * k:2 * k + 2, :], ps[:, 2 * (k % 2):2 * (k % 2) + 2, :], 0.0,
                                       mask[:, :].unsqueeze(1).broadcast_to([P, 2, T]), ALU.max, ALU.mult).then_inc(relu_done, 1)

            def step(f, b, last=False):
                if f is not None:
                    dve.wait_ge(idx_in, 16 * f + 16)
                    V.tensor_scalar(above[:, :], idx_sb[:, :], pos, -1.0, ALU.subtract, ALU.is_ge).then_inc(above_ready, 1)
                    dve.wait_ge(above_ready, f + 1)
                    V.scalar_tensor_tensor(mask[:, :], idx_sb[:, :], pos1, above[:, :], ALU.is_le, ALU.mult).then_inc(mask_ready, 1)
                if b is not None:
                    dve.wait_ge(xp_mm, b + 1)
                    V.tensor_tensor(xpT[:, :, :], ps[:, 2:4, :], xT_all[:, b, :, :], ALU.add).then_inc(xp_ready, 1)
                if f is not None:
                    dve.wait_ge(mask_ready, f + 1)
                    if not (isinstance(f, int) and f == 0):
                        dve.wait_ge(num_mm, f)
                    for k in range(4):
                        relu_mask(f, k)
                if b is not None:
                    dve.wait_ge(sc_mm, b + 1)
                    sc = ps[:, 7, :].rearrange("p (j n) -> p j n", n=P)[:, :, 0:K]
                    V.tensor_reduce(smax[:, :], sc, AX.X, ALU.max).then_inc(smax_ready, 1)
                    dve.wait_ge(smax_ready, b + 1)
                    V.tensor_tensor(sdiff[:, :, :], sc, smax[:, :].unsqueeze(2).broadcast_to([P, TT, K]),
                                    ALU.subtract).then_inc(sdiff_ready, 1)
                    dve.wait_ge(ex_ready, b + 1)
                    V.tensor_reduce(ssum[:, :], ex[:, :, :], AX.X, ALU.add).then_inc(ssum_ready, 1)
                    dve.wait_ge(ssum_ready, b + 1)
                    V.reciprocal(rsum[:, :], ssum[:, :]).then_inc(rsum_ready, 1)
                    dve.wait_ge(rsum_ready, b + 1)
                    V.tensor_tensor(en[:, :, 0:K], ex[:, :, :], rsum[:, :].unsqueeze(2).broadcast_to([P, TT, K]),
                                    ALU.mult).then_inc(en_ready, 1)
                if f is not None:
                    dve.wait_ge(denT_mm, f + 1)
                    dT = ps[:, 6, :].rearrange("p (j q r) -> p j q r", j=TT, q=4)
                    V.tensor_scalar(dmin[:, :], dT[:, :, 0, 4], 16.0 * EPS_DEN / D, 16.0 * EPS_DEN * EPS_RMS,
                                    ALU.mult, ALU.add).then_inc(dmin_ready, 1)
                    dve.wait_ge(dmin_ready, f + 1)
                    for g in range(DC):
                        i = V.tensor_tensor(dcl[:, :, HPH * g:HPH * (g + 1)].rearrange("p j (q i) -> p j q i", i=2),
                                            dT[:, :, :, 2 * g:2 * g + 2],
                                            dmin[:, :].unsqueeze(2).unsqueeze(3).broadcast_to([P, TT, 4, 2]), ALU.max)
                    i.then_inc(dcl_ready, 1)
                    dve.wait_ge(dcl_ready, f + 1)
                    V.reciprocal(rden[:, :, :], dcl[:, :, :]).then_inc(rden_ready, 1)
                    dve.wait_ge(rden_ready, f + 1)
                    V.tensor_copy(rexp[:, :, :].rearrange("p j (h d) -> p j h d", d=HD),
                                  rden[:, :, :].unsqueeze(3).broadcast_to([P, TT, H, HD])).then_inc(rexp_ready, 1)
                if b is not None:
                    dve.wait_ge(att_mm, b + 1)
                    V.tensor_tensor(zT[:, :, :], ps[:, 0:2, :], xpT[:, :, :], ALU.add).then_inc(z_ready, 1)
                if f is not None:
                    dve.wait_ge(rep_cp, f + 1)
                    dve.wait_ge(num_mm, f + 1)
                    V.tensor_tensor(oT[:, :, :], ps[:, 4:6, :], rep_sb[:, :, :], ALU.mult).then_inc(o_ready, 1)
                if b is not None:
                    dve.wait_ge(zt_mm, b + 1)
                    for j in range(TT):
                        i = V.bn_stats(stats[:, j, :], ps[:, 6 + j // 2, (j % 2) * D:(j % 2 + 1) * D])
                    i.then_inc(stats_ready, 1)
                    dve.wait_ge(stats_ready, b + 1)
                    mean_e, m2_e, mean_o, m2_o = (stats[:, :, i] for i in (1, 2, 4, 5))
                    V.tensor_tensor(mean_gap[:, :], mean_e, mean_o, ALU.subtract)
                    V.scalar_tensor_tensor(nmean2[:, :], mean_e, -1.0, mean_o, ALU.mult, ALU.subtract)
                    V.tensor_tensor(m2_sum[:, :], m2_e, m2_o, ALU.add).then_inc(parts_ready, 1)
                    dve.wait_ge(parts_ready, b + 1)
                    V.scalar_tensor_tensor(gap_sq[:, :], mean_gap[:, :], 0.25, mean_gap[:, :], ALU.mult, ALU.mult).then_inc(gap_ready, 1)
                    V.tensor_scalar(nmean[:, :], nmean2[:, :], 0.5, None, ALU.mult).then_inc(nmean_ready, 1)
                    dve.wait_ge(gap_ready, b + 1)
                    V.scalar_tensor_tensor(var[:, :], m2_sum[:, :], 1.0 / D, gap_sq[:, :], ALU.mult, ALU.add).then_inc(var_ready, 1)

            steps(dve, step)


def shape_constants():
    import numpy as np
    c = np.zeros((P, C_END), np.float32)
    r = np.arange(P)
    c[r, C_ID + r] = 1.0
    c[r, C_HEAD + r // HD] = 1.0
    c[r, C_HALF + r // K] = 1.0
    for s in range(2):
        c[r, C_DEN + 32 * s + 2 * s + r // K] = 1.0
    c[:, C_DEN + 64 + 4] = 1.0
    c[:, C_POS] = r % K
    c[:, C_POS + 1] = r % K + 1
    return c


def kernel(**inputs):
    import numpy as np
    import concourse.bacc as bacc
    from concourse.bass_utils import run_bass_kernel_spmd

    a = {k: np.asarray(v) for k, v in inputs.items()}

    def by_partition(v):
        return np.ascontiguousarray(v.reshape(DC, P).T)

    ctx = a["ctx_1024"].reshape(B * K, D)
    arrays = {
        "xT": a["x"].transpose(0, 2, 1), "ctx": ctx, "ctxT": ctx.T, "idx": a["itok_BxS_0_255"],
        "gq": by_partition(a["L0_xattn_gamma_q"]), "gkv": by_partition(a["L0_xattn_gamma_kv"]),
        "wq0T": a["L0_xattn_Wq"].T, "wk0T": a["L0_xattn_Wk"].T, "wv0T": a["L0_xattn_Wv"].T, "wo0T": a["L0_xattn_Wo"].T,
        "wq1": a["L1_xattn_Wq"], "bq1": by_partition(a["L1_xattn_bq"]),
        "wk1": a["L1_xattn_Wk"], "bk1": by_partition(a["L1_xattn_bk"]),
        "wv1": a["L1_xattn_Wv"], "bv1": by_partition(a["L1_xattn_bv"]),
        "wf1": a["L1_xattn_Wf"], "bf1": a["L1_xattn_bf"],
        "ln_g": a["L1_xattn_ln_gamma"], "ln_b": a["L1_xattn_ln_beta"],
        "consts": shape_constants(),
    }
    arrays = {k: np.ascontiguousarray(v) for k, v in arrays.items()}
    nc = bacc.Bacc("TRN2", target_bir_lowering=False, num_devices=1)
    args = [nc.dram_tensor(k, v.shape, mybir.dt.from_np(v.dtype), kind="ExternalInput").ap() for k, v in arrays.items()]
    args.append(nc.dram_tensor("out", (B, T, D), mybir.dt.float32, kind="ExternalOutput").ap())
    xattn_pair(nc, *args)
    r = run_bass_kernel_spmd(nc, [arrays], core_ids=[0])
    return r.results[0]["out"]
```

```python
import concourse.bass as bass
from concourse import mybir
from contextlib import ExitStack

B, T, D, K, H = 16, 512, 256, 64, 16
HD = D // H
P = 128
DC = D // P
TT = T // P
PAIRS = H // 2
HPH = H // DC
EPS_RMS = 1.1920929e-07
EPS_DEN = 1e-06
LN_EPS = 1e-05
CT = B * K // P
RING = 4

C_ID, C_HEAD, C_HALF, C_DEN, C_POS, C_END = 0, 128, 136, 138, 234, 236


def xattn_pair(nc: bass.Bass, xT, ctx, ctxT, idx, gq, gkv, wq0T, wk0T, wv0T, wo0T,
               wq1, bq1, wk1, bk1, wv1, bv1, wf1, bf1, ln_g, ln_b, consts, out):
    f32 = mybir.dt.float32
    f32r = mybir.dt.float32r
    i32 = mybir.dt.int32
    ALU = mybir.AluOpType
    ACT = mybir.ActivationFunctionType
    AX = mybir.AxisListType

    es = ExitStack()
    with es:
        def sb(name, shape, dt=f32):
            return es.enter_context(nc.sbuf_tensor(name, shape, dt))

        def sem(name):
            return es.enter_context(nc.semaphore(name))

        cst = sb("cst", [P, C_END])
        ident = cst[:, C_ID:C_ID + P]
        head_mask = cst[:, C_HEAD:C_HEAD + HPH]
        half_mask = cst[:, C_HALF:C_HALF + 2]
        den_sel = cst[:, C_DEN:C_DEN + 96].rearrange("p (s c) -> p s c", s=3)
        pos = cst[:, C_POS:C_POS + 1]
        pos1 = cst[:, C_POS + 1:C_POS + 2]
        vec = sb("vec", [P, 5, DC])
        bf_row = sb("bf_row", [P, D])
        lng_row = sb("lng_row", [P, D])
        lnb_row = sb("lnb_row", [P, D])
        minus_half = sb("minus_half", [P, CT])
        ln_eps = sb("ln_eps", [P, TT])
        zeros = sb("zeros", [P, D])
        x_ring = sb("x_ring", [P, RING, DC, T])
        idx_ring = sb("idx_ring", [P, RING, T], i32)
        v0d = sb("v0d", [P, B, D])
        vfd = sb("vfd", [P, B, D])
        k1T = sb("k1T", [P, DC, B * K + K])

        w_hi = {n: sb("wh_" + n, [P, DC, D], f32r) for n in ("q0", "o0", "q1")}
        w_lo = {n: sb("wl_" + n, [P, DC, D], f32r) for n in ("q0", "o0", "q1")}
        k0_hi = sb("k0_hi", [P, DC, B * K], f32r)
        k0_lo = sb("k0_lo", [P, DC, B * K], f32r)

        kb_hi = sb("kb_hi", [P, DC, HPH * K], f32r)
        kb_lo = sb("kb_lo", [P, DC, HPH * K], f32r)
        vblk = sb("vblk", [P, PAIRS, 2 * HD])
        vf_hi = sb("vf_hi", [P, D], f32r)
        vf_lo = sb("vf_lo", [P, D], f32r)
        above = sb("above", [P, T])
        mask = sb("mask", [P, T])
        x_hi = sb("x_hi", [P, DC, T], f32r)
        x_lo = sb("x_lo", [P, DC, T], f32r)
        q0_hi = sb("q0_hi", [P, DC, T], f32r)
        q0_lo = sb("q0_lo", [P, DC, T], f32r)
        w = sb("w", [P, PAIRS, T])
        den_sb = sb("den_sb", [P, T])
        dmin = sb("dmin", [P, TT])
        dcl = sb("dcl", [P, TT, H])
        rden = sb("rden", [P, TT, H])
        o_hi = sb("o_hi", [P, DC, T], f32r)
        o_lo = sb("o_lo", [P, DC, T], f32r)
        xp_hi = sb("xp_hi", [P, DC, T], f32r)
        xp_lo = sb("xp_lo", [P, DC, T], f32r)
        smax = sb("smax", [P, TT])
        sdiff = sb("sdiff", [P, TT, K])
        ex = sb("ex", [P, TT, K])
        ssum = sb("ssum", [P, TT])
        rsum = sb("rsum", [P, TT])
        enf = sb("enf", [P, TT, K])
        en = sb("en", [P, TT, 2, K], f32r)
        eT = sb("eT", [P, T], f32r)
        stats = sb("stats", [P, TT, 6])
        mean_gap, nmean2, m2_sum, gap_sq, var = (sb(n, [P, TT]) for n in ("mean_gap", "nmean2", "m2_sum", "gap_sq", "var"))
        veps = sb("veps", [P, TT])
        rstd = sb("rstd", [P, TT])
        nmean = sb("nmean", [P, TT])
        nbias = sb("nbias", [P, TT])
        bufs = sb("bufs", [P, 8, DC * T])
        xsq, rep_sb, oT, _, xpT, q1T, _, _ = (bufs[:, n, :].rearrange("p (c t) -> p c t", c=DC) for n in range(8))
        rexp, zn, zo = (bufs[:, n, :].rearrange("p (j d) -> p j d", j=TT) for n in (3, 6, 7))

        ctx_sb = w[:, 0:4, :].rearrange("p a b -> p (a b)").rearrange("p (t d) -> p t d", d=D)
        kn = w[:, 4:8, :].rearrange("p a b -> p (a b)").rearrange("p (t d) -> p t d", d=D)
        knT = bufs[:, 0:2, :]
        v0n = bufs[:, 2:4, :].rearrange("p a b -> p (a b)").rearrange("p (t d) -> p t d", d=D)
        v1T = bufs[:, 4:6, :]
        ctxT_sb = bufs[:, 6:8, :]
        vfn = bufs[:, 6:8, :].rearrange("p a b -> p (a b)").rearrange("p (t d) -> p t d", d=D)
        raw = {n: vfd[:, 2 * i:2 * i + 2, :] for i, n in enumerate(("k0", "v0", "k1", "v1", "f1", "q0", "o0", "q1"))}
        csq = x_ring[:, RING - 1, 0, 0:D]
        cms = sb("cms", [P, CT])
        cmean = sb("cmean", [P, CT])
        crs = sb("crs", [P, CT])

        ps = es.enter_context(nc.psum_tensor("ps", [P, 8, 512], f32))

        consts_in, ctx_in, ctxT_in, wk1_in, wv1_in, w0_in, w1_in, x_in, idx_in = map(sem, (
            "consts_in", "ctx_in", "ctxT_in", "wk1_in", "wv1_in", "w0_in", "w1_in", "x_in", "idx_in"))
        folded, weights_hi, weights_ready, cms_done, cmean_done, crs_done, kn_done, knT_mm, knT_cp, half_set, k1_padded = map(sem, (
            "folded", "weights_hi", "weights_ready", "cms_done", "cmean_done", "crs_done", "kn_done", "knT_mm", "knT_cp",
            "half_set", "k1_padded"))
        prep_mm, prep_act, prep_dve, k0h_cp, v0d_in, vfd_in = map(sem, (
            "prep_mm", "prep_act", "prep_dve", "k0h_cp", "v0d_in", "vfd_in"))
        kblk_ready, vblk_ready, vfh_ready, vf_ready = map(sem, ("kblk_ready", "vblk_ready", "vfh_ready", "vf_ready"))
        above_ready, mask_ready, xsq_ready, xh_ready, xl_ready = map(sem, (
            "above_ready", "mask_ready", "xsq_ready", "xh_ready", "xl_ready"))
        q0_mm, q0h_ready, q0l_ready, s_mm, relu_done, w_ready = map(sem, (
            "q0_mm", "q0h_ready", "q0l_ready", "s_mm", "relu_done", "w_ready"))
        den_mm, num_mm, den_cp, denT_mm, dmin_ready, dcl_ready, rden_ready = map(sem, (
            "den_mm", "num_mm", "den_cp", "denT_mm", "dmin_ready", "dcl_ready", "rden_ready"))
        rexp_ready, rep_mm, rep_cp, o_ready, oh_ready, ol_ready = map(sem, (
            "rexp_ready", "rep_mm", "rep_cp", "o_ready", "oh_ready", "ol_ready"))
        xp_mm, xp_ready, xph_ready, xpl_ready, q1_mm, q1_ready, sc_mm = map(sem, (
            "xp_mm", "xp_ready", "xph_ready", "xpl_ready", "q1_mm", "q1_ready", "sc_mm"))
        smax_ready, sdiff_ready, ex_ready, ssum_ready, rsum_ready, enf_ready, enh_ready, en_ready = map(sem, (
            "smax_ready", "sdiff_ready", "ex_ready", "ssum_ready", "rsum_ready", "enf_ready", "enh_ready", "en_ready"))
        eT_mm, eT_ready, z_mm = map(sem, ("eT_mm", "eT_ready", "z_mm"))
        stats_ready, parts_ready, gap_ready, var_ready, veps_ready, rstd_ready, nmean_ready, nbias_ready = map(sem, (
            "stats_ready", "parts_ready", "gap_ready", "var_ready", "veps_ready", "rstd_ready", "nmean_ready", "nbias_ready"))
        zn_ready, zg_ready, zo_ready, out_done = map(sem, ("zn_ready", "zg_ready", "zo_ready", "out_done"))

        block = es.enter_context(nc.Block())

        FIRST_STEADY, LAST_STEADY = 2, B - 1

        def steps(engine, step):
            step(0, None, None)
            step(1, 0, None)
            with engine.Fori(FIRST_STEADY, LAST_STEADY) as i:
                step(i, i - 1, i - 2)
            step(B - 1, B - 2, B - 3, last=True)
            step(None, B - 1, B - 2)
            step(None, None, B - 1)

        def steps_turned(engine, head, tail):
            head(0, None)
            tail(0, None)
            head(1, 0)
            tail(1, 0)
            head(FIRST_STEADY, FIRST_STEADY - 1)
            with engine.Fori(FIRST_STEADY, LAST_STEADY) as i:
                tail(i, i - 1)
                head(i + 1, i)
            tail(B - 1, B - 2, last=True)
            head(None, B - 1)
            tail(None, B - 1)

        def first(n):
            return isinstance(n, int) and n == 0

        def f32_view(t):
            return t.bitcast(f32)

        RESULTS = ["act"] * 4 + ["act"] * 4 + ["dve"] * 4 + ["act"] * CT + ["dve"] * CT
        K1, V1, K0, V0, VF = 0, 4, 8, 12, 12 + CT

        def copied_until(n, engine):
            return sum(e == engine for e in RESULTS[:n + 1])

        @block.sync
        def _(sp):
            def weight(name, src, done):
                sp.dma_start(raw[name], src.rearrange("(c p) e -> p c e", p=P)).then_inc(done, 16)

            def load(i):
                sp.dma_start(x_ring[:, i % RING, :, :], xT[i].rearrange("(c p) t -> p c t", p=P)).then_inc(x_in, 16)
                sp.dma_start(idx_ring[:, i % RING, :], idx[i].partition_broadcast(P)).then_inc(idx_in, 16)

            for i, v in enumerate((gq, gkv, bq1, bk1, bv1)):
                sp.dma_start(vec[:, i, :], v).then_inc(consts_in, 16)
            sp.dma_start(cst[:, :], consts).then_inc(consts_in, 16)
            weight("k1", wk1, wk1_in)
            sp.dma_start(ctxT_sb, ctxT.rearrange("(c p) n -> p c n", p=P)).then_inc(ctxT_in, 16)
            sp.dma_start(ctx_sb, ctx.rearrange("(t p) d -> p t d", p=P)).then_inc(ctx_in, 16)
            weight("v1", wv1, wv1_in)
            weight("k0", wk0T, w0_in)
            weight("v0", wv0T, w0_in)
            weight("q0", wq0T, w0_in)
            load(0)
            weight("f1", wf1, w1_in)
            weight("o0", wo0T, w1_in)
            weight("q1", wq1, w1_in)
            for t, v in ((bf_row, bf1), (lng_row, ln_g), (lnb_row, ln_b)):
                sp.dma_start(t[:, :], v.partition_broadcast(P)).then_inc(w1_in, 16)
            sp.wait_ge(prep_act, copied_until(VF - 1, "act"))
            for half in range(2):
                for odd in range(2):
                    sp.dma_start(v0d[half * K:(half + 1) * K, odd::2, :], v0n[odd * K:(odd + 1) * K, :, :]).then_inc(v0d_in, 16)
            sp.wait_ge(x_in, 16)
            sp.wait_ge(idx_in, 16)
            load(1)
            sp.wait_ge(prep_dve, copied_until(VF + CT - 1, "dve"))
            sp.wait_ge(weights_ready, 3)
            for half in range(2):
                for odd in range(2):
                    sp.dma_start(vfd[half * K:(half + 1) * K, odd::2, :], vfn[odd * K:(odd + 1) * K, :, :]).then_inc(vfd_in, 16)
            for i in range(2, RING):
                sp.wait_ge(x_in, 16 * i)
                sp.wait_ge(idx_in, 16 * i)
                load(i)
            with sp.Fori(1, B - RING + 1) as read:
                sp.wait_ge(xp_ready, 2 * read)
                sp.wait_ge(mask_ready, read)
                sp.wait_ge(x_in, 16 * read + 16 * (RING - 1))
                sp.wait_ge(idx_in, 16 * read + 16 * (RING - 1))
                load(read + (RING - 1))

        @block.gpsimd
        def _(pool):
            G = nc.gpsimd
            G.memset(minus_half[:, :], -0.5).then_inc(half_set, 1)
            G.memset(ln_eps[:, :], LN_EPS).then_inc(half_set, 1)
            G.memset(zeros[:, :], 0.0).then_inc(half_set, 1)
            G.memset(k1T[:, :, B * K:], 0.0).then_inc(k1_padded, 1)
            pool.wait_ge(cms_done, CT)
            G.tensor_scalar(cmean[:, :], cms[:, :], 1.0 / D, EPS_RMS, ALU.mult, ALU.add).then_inc(cmean_done, 1)
            pool.wait_ge(cmean_done, 1)
            pool.wait_ge(half_set, 3)
            G.tensor_tensor(crs[:, :], cmean[:, :], minus_half[:, :], ALU.pow).then_inc(crs_done, 1)

            def build_kblk(f):
                for table, blk in ((k0_hi, kb_hi), (k0_lo, kb_lo)):
                    for g in range(DC):
                        i = G.tensor_tensor(blk[:, g, :].rearrange("p (h k) -> p h k", k=K),
                                            f32_view(table[:, g, bass.ts(f, K)]).unsqueeze(1).broadcast_to([P, HPH, K]),
                                            head_mask.unsqueeze(2).broadcast_to([P, HPH, K]), ALU.mult)
                i.then_inc(kblk_ready, 1)

            def build_vblk(f):
                G.tensor_tensor(vblk[:, :, :].rearrange("p c (j d) -> p c j d", j=2),
                                v0d[:, f, :].rearrange("p (c j d) -> p c j d", j=2, d=HD),
                                half_mask.unsqueeze(1).unsqueeze(3).broadcast_to([P, PAIRS, 2, HD]),
                                ALU.mult).then_inc(vblk_ready, 1)

            def split_x_lo(f):
                pool.wait_ge(xh_ready, 2 * f + 2)
                G.tensor_tensor(x_lo[:, :, :], x_ring[:, f % RING, :, :], f32_view(x_hi[:, :, :]), ALU.subtract).then_inc(xl_ready, 2)

            pool.wait_ge(consts_in, 16 * 6)
            split_x_lo(0)
            pool.wait_ge(prep_dve, copied_until(V0 - 1, "dve"))
            build_kblk(0)
            pool.wait_ge(v0d_in, 16 * 4)
            build_vblk(0)

            def step(f, b, n, last=False):
                if n is not None:
                    pool.wait_ge(var_ready, n + 1)
                    G.tensor_tensor(veps[:, :], var[:, :], ln_eps[:, :], ALU.add).then_inc(veps_ready, 1)
                    pool.wait_ge(veps_ready, n + 1)
                    G.tensor_tensor(rstd[:, :], veps[:, :], minus_half[:, 0:TT], ALU.pow).then_inc(rstd_ready, 1)
                    pool.wait_ge(rstd_ready, n + 1)
                    pool.wait_ge(nmean_ready, n + 1)
                    G.tensor_tensor(nbias[:, :], nmean[:, :], rstd[:, :], ALU.mult).then_inc(nbias_ready, 1)
                if f is not None and not last:
                    split_x_lo(f + 1)
                if n is not None:
                    pool.wait_ge(zn_ready, n + 1)
                    if not first(n):
                        pool.wait_ge(out_done, 16 * n)
                    G.tensor_tensor(zo, zn, lng_row[:, :].unsqueeze(1).broadcast_to([P, TT, D]), ALU.mult).then_inc(zg_ready, 1)
                    pool.wait_ge(zg_ready, n + 1)
                    G.tensor_tensor(zo, zo, lnb_row[:, :].unsqueeze(1).broadcast_to([P, TT, D]), ALU.add).then_inc(zo_ready, 1)
                    pool.wait_ge(zo_ready, n + 1)
                    pool.dma_start(out[n].rearrange("(j p) d -> p j d", p=P), zo).then_inc(out_done, 16)
                if f is not None and not last:
                    pool.wait_ge(s_mm, 4 * f + 4)
                    build_kblk(f + 1)
                    pool.wait_ge(num_mm, f + 1)
                    build_vblk(f + 1)
                if f is not None:
                    if b is not None:
                        pool.wait_ge(z_mm, b + 1)
                    else:
                        pool.wait_ge(vfd_in, 16 * 4)
                    G.tensor_tensor(vf_hi[:, :], vfd[:, f, :], zeros[:, :], ALU.add).then_inc(vfh_ready, 1)

            steps(pool, step)
            pool.wait_ge(out_done, 16 * B)

        @block.tensor
        def _(pe):
            mm = nc.tensor.matmul

            def result(n, parts):
                if n >= 4:
                    owner = RESULTS[n - 4]
                    pe.wait_ge(prep_act if owner == "act" else prep_dve, copied_until(n - 4, owner))
                for i, (stationary, moving, cols) in enumerate(parts):
                    last = mm(ps[:, 4 + n % 4, 0:cols], stationary, moving, start=(i == 0), stop=(i == len(parts) - 1))
                last.then_inc(prep_mm, 1)

            def transposed(n0, name, src):
                for e in range(DC):
                    for n in range(2):
                        result(n0 + 2 * e + n, [(raw[name][:, c, e * P:(e + 1) * P], src[:, c, n * 512:(n + 1) * 512], 512)
                                                for c in range(DC)])

            pe.wait_ge(wk1_in, 16)
            pe.wait_ge(ctxT_in, 16)
            transposed(K1, "k1", ctxT_sb)
            pe.wait_ge(wv1_in, 16)
            transposed(V1, "v1", ctxT_sb)
            pe.wait_ge(consts_in, 16 * 6)
            for t in range(CT):
                pe.wait_ge(kn_done, t + 1)
                if t >= 4:
                    pe.wait_ge(knT_cp, t - 3)
                for c in range(DC):
                    last = nc.tensor.transpose(ps[:, t % 4, c * P:(c + 1) * P], kn[:, t, c * P:(c + 1) * P], ident)
                last.then_inc(knT_mm, 1)
            pe.wait_ge(knT_cp, CT)
            pe.wait_ge(folded, 3)
            transposed(K0, "k0", knT)
            for t in range(CT):
                result(V0 + t, [(knT[:, c, t * P:(t + 1) * P], raw["v0"][:, c, :], D) for c in range(DC)])
            pe.wait_ge(w1_in, 16 * 6)
            pe.wait_ge(prep_act, copied_until(K0 - 1, "act"))
            for t in range(CT):
                result(VF + t, [(v1T[:, c, t * P:(t + 1) * P], raw["f1"][:, c, :], D) for c in range(DC)])
            pe.wait_ge(prep_dve, copied_until(VF + CT - 1, "dve"))
            pe.wait_ge(weights_ready, 3)
            pe.wait_ge(k1_padded, 1)

            def project(bank0, name, m_hi, m_lo, ready_hi, ready_lo, i, done):
                for c in range(DC):
                    pe.wait_ge(ready_hi, 2 * i + c + 1)
                    pe.wait_ge(ready_lo, 2 * i + c + 1)
                    for e in range(DC):
                        o = ps[:, bank0 + e, :]
                        hi, lo = (t[name][:, c, e * P:(e + 1) * P] for t in (w_hi, w_lo))
                        mm(o, hi, m_hi[:, c, :], start=(c == 0), stop=False)
                        mm(o, lo, m_hi[:, c, :], start=False, stop=False)
                        last = mm(o, hi, m_lo[:, c, :], start=False, stop=(c == DC - 1))
                        if c == DC - 1:
                            last.then_inc(done, 1)

            def scores(f, b, pairs):
                for c in pairs:
                    if c < DC:
                        pe.wait_ge(q0h_ready, 2 * f + c + 1)
                        pe.wait_ge(q0l_ready, 2 * f + c + 1)
                    if c == 2 and b is not None:
                        pe.wait_ge(xp_ready, 2 * b + 2)
                    if c >= 4 and c % 2 == 0:
                        pe.wait_ge(relu_done, 4 * f + (c - 4) // 2 + 1)
                    cols = slice((c % 4) * P, (c % 4 + 1) * P)
                    o, g = ps[:, c % 4, :], c // 4
                    mm(o, kb_hi[:, g, cols], q0_hi[:, g, :], start=True, stop=False)
                    mm(o, kb_lo[:, g, cols], q0_hi[:, g, :], start=False, stop=False)
                    last = mm(o, kb_hi[:, g, cols], q0_lo[:, g, :], start=False, stop=True)
                    if c % 2:
                        last.then_inc(s_mm, 1)

            def step(f, b, n, last=False):
                if f is not None:
                    project(0, "q0", x_hi, x_lo, xh_ready, xl_ready, f, q0_mm)
                if b is not None:
                    project(2, "o0", o_hi, o_lo, oh_ready, ol_ready, b, xp_mm)
                if f is not None:
                    pe.wait_ge(kblk_ready, f + 1)
                    scores(f, b, range(PAIRS))
                if b is not None:
                    if not first(b):
                        pe.wait_ge(zn_ready, b)
                    project(6, "q1", xp_hi, xp_lo, xph_ready, xpl_ready, b, q1_mm)

                def numerators(g):
                    for q in range(4):
                        i = mm(ps[32 * q:32 * q + 32, 4 + g, :], vblk[:, 4 * g + q, :], w[:, 4 * g + q, :],
                               start=True, stop=True)
                    return i

                def denominators(g):
                    for q in range(4):
                        i = mm(ps[32 * q:32 * q + 32, 0, :], den_sel[:, g, :], w[:, 4 * g + q, :],
                               start=(g == 0), stop=(g == DC - 1 and q > 0))
                    return i

                if f is not None:
                    pe.wait_ge(vblk_ready, f + 1)
                    if b is not None:
                        pe.wait_ge(o_ready, 2 * b + 2)
                    pe.wait_ge(w_ready, 4 * f + 2)
                    numerators(0)
                    pe.wait_ge(relu_done, 4 * f + 3)
                    denominators(0)
                if b is not None:
                    pe.wait_ge(q1_ready, b + 1)
                    for j in range(TT):
                        for c in range(DC):
                            i = mm(ps[:, 7, j * P:(j + 1) * P], q1T[:, c, j * P:(j + 1) * P],
                                   k1T[:, c, bass.ds(b * K, 2 * K)], start=(c == 0), stop=(c == DC - 1))
                    i.then_inc(sc_mm, 1)
                if f is not None:
                    pe.wait_ge(w_ready, 4 * f + 4)
                    denominators(1)
                    pe.wait_ge(xsq_ready, f + 1)
                    for c in range(DC):
                        i = mm(ps[0:32, 0, :], den_sel[:, 2, :], xsq[:, c, :], start=False, stop=(c == DC - 1))
                    i.then_inc(den_mm, 1)
                    numerators(1).then_inc(num_mm, 1)
                    pe.wait_ge(den_cp, f + 1)
                    for j in range(TT):
                        i = nc.tensor.transpose(ps[:, 0, j * P:(j + 1) * P], den_sb[:, j * P:(j + 1) * P], ident)
                    i.then_inc(denT_mm, 1)

                def back(j):
                    for c in range(DC):
                        at = (j % 2) * D + c * P
                        mm(ps[:, 6 + j // 2, at:at + P], xpT[:, c, j * P:(j + 1) * P], ident,
                           is_transpose=True, start=(at == 0), stop=False, skip_group_check=True)

                if b is not None:
                    back(0)
                    back(1)
                    pe.wait_ge(en_ready, b + 1)
                    for j in range(TT):
                        i = nc.tensor.transpose(ps[:, 7, j * P:(j + 1) * P],
                                                f32_view(en[:, j, :, :]).rearrange("p a k -> p (a k)"), ident)
                    i.then_inc(eT_mm, 1)
                    pe.wait_ge(eT_ready, b + 1)
                    back(2)
                    back(3)
                if f is not None:
                    pe.wait_ge(rexp_ready, f + 1)
                    for g in range(DC):
                        for j in range(TT):
                            i = nc.tensor.transpose(ps[:, 2 + g, j * P:(j + 1) * P], rexp[:, j, g * P:(g + 1) * P], ident)
                        i.then_inc(rep_mm, 1)
                if b is not None:
                    pe.wait_ge(vf_ready, b + 1)
                    for j in range(TT):
                        at = (j % 2) * D
                        for part in (vf_hi, vf_lo):
                            i = mm(ps[:, 6 + j // 2, at:at + D], eT[:, j * P:(j + 1) * P], part[:, :],
                                   start=False, stop=(part is vf_lo), skip_group_check=True)
                    i.then_inc(z_mm, 1)

            steps(pe, step)

        @block.scalar
        def _(act):
            A = nc.scalar.activation
            act.wait_ge(consts_in, 16 * 6)
            act.wait_ge(ctx_in, 16)
            for t in range(CT):
                if t:
                    act.wait_ge(cms_done, t)
                A(csq, ctx_sb[:, t, :], ACT.Square, accum_out=cms[:, t:t + 1]).then_inc(cms_done, 1)

            def copy_out(n, dst, cols, func, **kw):
                act.wait_ge(prep_mm, n + 1)
                return A(dst, ps[:, 4 + n % 4, 0:cols], func, **kw)

            for n0, dst, bias in ((K1, k1T, 3), (V1, v1T, 4)):
                for e in range(DC):
                    for h in range(2):
                        copy_out(n0 + 2 * e + h, dst[:, e, h * 512:(h + 1) * 512], 512, ACT.Gelu,
                                 bias=vec[:, bias, e:e + 1]).then_inc(prep_act, 1)
            for t in range(CT):
                act.wait_ge(knT_mm, t + 1)
                A(knT[:, :, t * P:(t + 1) * P], ps[:, t % 4, 0:D].rearrange("p (c n) -> p c n", c=DC), ACT.Copy).then_inc(knT_cp, 1)
            for e in range(DC):
                for h in range(2):
                    copy_out(K0 + 2 * e + h, k0_hi[:, e, h * 512:(h + 1) * 512], 512, ACT.Copy).then_inc(k0h_cp, 1)
            for t in range(CT):
                copy_out(V0 + t, v0n[:, t, :], D, ACT.Copy).then_inc(prep_act, 1)

            def split_x_hi(f):
                act.wait_ge(x_in, 16 * f + 16)
                if not first(f):
                    act.wait_ge(q0_mm, 2 * f)
                A(x_hi[:, :, :], x_ring[:, f % RING, :, :], ACT.Copy).then_inc(xh_ready, 2)

            def square(f, k):
                act.wait_ge(relu_done, 4 * f + k + 1)
                A(w[:, 2 * k:2 * k + 2, :], w[:, 2 * k:2 * k + 2, :], ACT.Square).then_inc(w_ready, 1)

            split_x_hi(0)

            def step(f, b, n, last=False):
                if f is not None:
                    for g in range(DC):
                        act.wait_ge(q0_mm, 2 * f + g + 1)
                        A(q0_hi[:, g, :], ps[:, g, :], ACT.Copy).then_inc(q0h_ready, 1)
                    if not last:
                        split_x_hi(f + 1)
                    if not first(f):
                        act.wait_ge(den_mm, f)
                    A(xsq, x_ring[:, f % RING, :, :], ACT.Square).then_inc(xsq_ready, 1)
                if n is not None:
                    act.wait_ge(z_mm, n + 1)
                    act.wait_ge(nbias_ready, n + 1)
                    if not first(n):
                        act.wait_ge(zg_ready, n)
                    for j in range(TT):
                        i = A(zn[:, j, :], ps[:, 6 + j // 2, (j % 2) * D:(j % 2 + 1) * D], ACT.Identity,
                              bias=nbias[:, j:j + 1], scale=rstd[:, j:j + 1])
                    i.then_inc(zn_ready, 1)
                if b is not None:
                    for g in range(DC):
                        act.wait_ge(xp_ready, 2 * b + g + 1)
                        A(xp_hi[:, g, :], xpT[:, g, :], ACT.Copy).then_inc(xph_ready, 1)
                if f is not None:
                    square(f, 0)
                    square(f, 1)
                if b is not None:
                    for e in range(DC):
                        act.wait_ge(q1_mm, 2 * b + e + 1)
                        i = A(q1T[:, e, :], ps[:, 6 + e, :], ACT.Gelu, bias=vec[:, 2, e:e + 1])
                    i.then_inc(q1_ready, 1)
                if f is not None:
                    square(f, 2)
                    square(f, 3)
                if b is not None:
                    act.wait_ge(sdiff_ready, b + 1)
                    A(ex[:, :, :], sdiff[:, :, :], ACT.Exp).then_inc(ex_ready, 1)
                if f is not None:
                    act.wait_ge(den_mm, f + 1)
                    A(den_sb[:, :], ps[:, 0, :], ACT.Copy).then_inc(den_cp, 1)
                if b is not None:
                    act.wait_ge(eT_mm, b + 1)
                    A(eT[:, :], ps[:, 7, :], ACT.Copy).then_inc(eT_ready, 1)
                if f is not None:
                    for g in range(DC):
                        act.wait_ge(rep_mm, 2 * f + g + 1)
                        A(rep_sb[:, g, :], ps[:, 2 + g, :], ACT.Copy).then_inc(rep_cp, 1)
                    for g in range(DC):
                        act.wait_ge(o_ready, 2 * f + g + 1)
                        A(o_hi[:, g, :], oT[:, g, :], ACT.Copy).then_inc(oh_ready, 1)

            steps(act, step)

        @block.vector
        def _(dve):
            V = nc.vector
            dve.wait_ge(consts_in, 16 * 6)
            dve.wait_ge(w0_in, 16 * 3)
            for n, g in (("k0", 1), ("v0", 1), ("q0", 0)):
                for c in range(DC):
                    last = V.tensor_scalar(raw[n][:, c, :], raw[n][:, c, :], vec[:, g, c:c + 1], None, ALU.mult)
                last.then_inc(folded, 1)
            dve.wait_ge(crs_done, 1)
            for t in range(CT):
                V.tensor_scalar(kn[:, t, :], ctx_sb[:, t, :], crs[:, t:t + 1], None, ALU.mult).then_inc(kn_done, 1)
            dve.wait_ge(w1_in, 16 * 6)
            dve.wait_ge(folded, 3)
            for i, n in enumerate(("q0", "o0", "q1")):
                V.tensor_copy(w_hi[n][:, :, :], raw[n]).then_inc(weights_hi, 1)
                dve.wait_ge(weights_hi, i + 1)
                V.tensor_tensor(w_lo[n][:, :, :], raw[n], f32_view(w_hi[n][:, :, :]), ALU.subtract).then_inc(weights_ready, 1)
            for e in range(DC):
                for h in range(2):
                    dve.wait_ge(k0h_cp, 2 * e + h + 1)
                    V.tensor_tensor(k0_lo[:, e, h * 512:(h + 1) * 512], ps[:, 4 + (K0 + 2 * e + h) % 4, :],
                                    f32_view(k0_hi[:, e, h * 512:(h + 1) * 512]), ALU.subtract).then_inc(prep_dve, 1)
            for t in range(CT):
                dve.wait_ge(prep_mm, VF + t + 1)
                V.tensor_tensor(vfn[:, t, :], ps[:, 4 + (VF + t) % 4, 0:D], bf_row[:, :], ALU.add).then_inc(prep_dve, 1)

            def build_mask(f):
                dve.wait_ge(idx_in, 16 * f + 16)
                V.tensor_scalar(above[:, :], idx_ring[:, f % RING, :], pos, -1.0, ALU.subtract, ALU.is_ge).then_inc(above_ready, 1)
                dve.wait_ge(above_ready, f + 1)
                V.scalar_tensor_tensor(mask[:, :], idx_ring[:, f % RING, :], pos1, above[:, :], ALU.is_le, ALU.mult).then_inc(mask_ready, 1)

            build_mask(0)

            def relu_mask(f, k):
                dve.wait_ge(s_mm, 4 * f + k + 1)
                V.scalar_tensor_tensor(w[:, 2 * k:2 * k + 2, :], ps[:, 2 * (k % 2):2 * (k % 2) + 2, :], 0.0,
                                       mask[:, :].unsqueeze(1).broadcast_to([P, 2, T]), ALU.max, ALU.mult).then_inc(relu_done, 1)

            def head(f, b):
                if f is not None:
                    for g in range(DC):
                        dve.wait_ge(q0h_ready, 2 * f + g + 1)
                        V.tensor_tensor(q0_lo[:, g, :], ps[:, g, :], f32_view(q0_hi[:, g, :]), ALU.subtract).then_inc(q0l_ready, 1)
                if b is not None:
                    for g in range(DC):
                        dve.wait_ge(xp_mm, 2 * b + g + 1)
                        V.tensor_tensor(xpT[:, g, :], ps[:, 2 + g, :], x_ring[:, b % RING, g, :], ALU.add).then_inc(xp_ready, 1)
                if f is not None:
                    dve.wait_ge(mask_ready, f + 1)
                    if not first(f):
                        dve.wait_ge(num_mm, f)
                    relu_mask(f, 0)
                    relu_mask(f, 1)
                if b is not None:
                    dve.wait_ge(vfh_ready, b + 1)
                    V.tensor_tensor(vf_lo[:, :], vfd[:, b, :], f32_view(vf_hi[:, :]), ALU.subtract).then_inc(vf_ready, 1)
                    for g in range(DC):
                        dve.wait_ge(xph_ready, 2 * b + g + 1)
                        V.tensor_tensor(xp_lo[:, g, :], xpT[:, g, :], f32_view(xp_hi[:, g, :]), ALU.subtract).then_inc(xpl_ready, 1)
                if f is not None:
                    relu_mask(f, 2)
                    relu_mask(f, 3)

            def tail(f, b, last=False):
                if f is not None and not last:
                    build_mask(f + 1)
                if b is not None:
                    dve.wait_ge(sc_mm, b + 1)
                    sc = ps[:, 7, :].rearrange("p (j n) -> p j n", n=P)[:, :, 0:K]

                    def per_row(t):
                        return t[:, :].unsqueeze(2).broadcast_to([P, TT, K])

                    V.tensor_reduce(smax[:, :], sc, AX.X, ALU.max).then_inc(smax_ready, 1)
                    dve.wait_ge(smax_ready, b + 1)
                    V.tensor_tensor(sdiff[:, :, :], sc, per_row(smax), ALU.subtract).then_inc(sdiff_ready, 1)
                    dve.wait_ge(ex_ready, b + 1)
                    V.tensor_reduce(ssum[:, :], ex[:, :, :], AX.X, ALU.add).then_inc(ssum_ready, 1)
                    dve.wait_ge(ssum_ready, b + 1)
                    V.reciprocal(rsum[:, :], ssum[:, :]).then_inc(rsum_ready, 1)
                    dve.wait_ge(rsum_ready, b + 1)
                    V.tensor_tensor(enf[:, :, :], ex[:, :, :], per_row(rsum), ALU.mult).then_inc(enf_ready, 1)
                    dve.wait_ge(enf_ready, b + 1)
                    V.tensor_copy(en[:, :, 0, :], enf[:, :, :]).then_inc(enh_ready, 1)
                    dve.wait_ge(enh_ready, b + 1)
                    V.tensor_tensor(en[:, :, 1, :], enf[:, :, :], f32_view(en[:, :, 0, :]), ALU.subtract).then_inc(en_ready, 1)
                if f is not None:
                    dve.wait_ge(denT_mm, f + 1)
                    dT = ps[:, 0, :].rearrange("p (j q r) -> p j q r", j=TT, q=4)
                    V.tensor_scalar(dmin[:, :], dT[:, :, 0, 4], 16.0 * EPS_DEN / D, 16.0 * EPS_DEN * EPS_RMS,
                                    ALU.mult, ALU.add).then_inc(dmin_ready, 1)
                    dve.wait_ge(dmin_ready, f + 1)
                    for g in range(DC):
                        i = V.tensor_tensor(dcl[:, :, HPH * g:HPH * (g + 1)].rearrange("p j (q i) -> p j q i", i=2),
                                            dT[:, :, :, 2 * g:2 * g + 2],
                                            dmin[:, :].unsqueeze(2).unsqueeze(3).broadcast_to([P, TT, 4, 2]), ALU.max)
                    i.then_inc(dcl_ready, 1)
                    dve.wait_ge(dcl_ready, f + 1)
                    V.reciprocal(rden[:, :, :], dcl[:, :, :]).then_inc(rden_ready, 1)
                    dve.wait_ge(rden_ready, f + 1)
                    V.tensor_copy(rexp.rearrange("p j (h d) -> p j h d", d=HD),
                                  rden[:, :, :].unsqueeze(3).broadcast_to([P, TT, H, HD])).then_inc(rexp_ready, 1)
                    dve.wait_ge(num_mm, f + 1)
                    for g in range(DC):
                        dve.wait_ge(rep_cp, 2 * f + g + 1)
                        V.tensor_tensor(oT[:, g, :], ps[:, 4 + g, :], rep_sb[:, g, :], ALU.mult).then_inc(o_ready, 1)
                    for g in range(DC):
                        dve.wait_ge(oh_ready, 2 * f + g + 1)
                        V.tensor_tensor(o_lo[:, g, :], oT[:, g, :], f32_view(o_hi[:, g, :]), ALU.subtract).then_inc(ol_ready, 1)
                if b is not None:
                    dve.wait_ge(z_mm, b + 1)
                    for j in range(TT):
                        i = V.bn_stats(stats[:, j, :], ps[:, 6 + j // 2, (j % 2) * D:(j % 2 + 1) * D])
                    i.then_inc(stats_ready, 1)
                    dve.wait_ge(stats_ready, b + 1)
                    mean_e, m2_e, mean_o, m2_o = (stats[:, :, i] for i in (1, 2, 4, 5))
                    V.tensor_tensor(mean_gap[:, :], mean_e, mean_o, ALU.subtract)
                    V.scalar_tensor_tensor(nmean2[:, :], mean_e, -1.0, mean_o, ALU.mult, ALU.subtract)
                    V.tensor_tensor(m2_sum[:, :], m2_e, m2_o, ALU.add).then_inc(parts_ready, 1)
                    dve.wait_ge(parts_ready, b + 1)
                    V.scalar_tensor_tensor(gap_sq[:, :], mean_gap[:, :], 0.25, mean_gap[:, :], ALU.mult, ALU.mult).then_inc(gap_ready, 1)
                    V.tensor_scalar(nmean[:, :], nmean2[:, :], 0.5, None, ALU.mult).then_inc(nmean_ready, 1)
                    dve.wait_ge(gap_ready, b + 1)
                    V.scalar_tensor_tensor(var[:, :], m2_sum[:, :], 1.0 / D, gap_sq[:, :], ALU.mult, ALU.add).then_inc(var_ready, 1)

            steps_turned(dve, head, tail)


def shape_constants():
    import numpy as np
    c = np.zeros((P, C_END), np.float32)
    r = np.arange(P)
    c[r, C_ID + r] = 1.0
    c[r, C_HEAD + r // HD] = 1.0
    c[r, C_HALF + r // K] = 1.0
    for s in range(2):
        c[r, C_DEN + 32 * s + 2 * s + r // K] = 1.0
    c[:, C_DEN + 64 + 4] = 1.0
    c[:, C_POS] = r % K
    c[:, C_POS + 1] = r % K + 1
    return c


def kernel(**inputs):
    import numpy as np
    import concourse.bacc as bacc
    from concourse.bass_utils import run_bass_kernel_spmd

    a = {k: np.asarray(v) for k, v in inputs.items()}

    def by_partition(v):
        return np.ascontiguousarray(v.reshape(DC, P).T)

    ctx = a["ctx_1024"].reshape(B * K, D)
    arrays = {
        "xT": a["x"].transpose(0, 2, 1), "ctx": ctx, "ctxT": ctx.T, "idx": a["itok_BxS_0_255"],
        "gq": by_partition(a["L0_xattn_gamma_q"]), "gkv": by_partition(a["L0_xattn_gamma_kv"]),
        "wq0T": a["L0_xattn_Wq"].T, "wk0T": a["L0_xattn_Wk"].T, "wv0T": a["L0_xattn_Wv"].T, "wo0T": a["L0_xattn_Wo"].T,
        "wq1": a["L1_xattn_Wq"], "bq1": by_partition(a["L1_xattn_bq"]),
        "wk1": a["L1_xattn_Wk"], "bk1": by_partition(a["L1_xattn_bk"]),
        "wv1": a["L1_xattn_Wv"], "bv1": by_partition(a["L1_xattn_bv"]),
        "wf1": a["L1_xattn_Wf"], "bf1": a["L1_xattn_bf"],
        "ln_g": a["L1_xattn_ln_gamma"], "ln_b": a["L1_xattn_ln_beta"],
        "consts": shape_constants(),
    }
    arrays = {k: np.ascontiguousarray(v) for k, v in arrays.items()}
    nc = bacc.Bacc("TRN2", target_bir_lowering=False, num_devices=1)
    args = [nc.dram_tensor(k, v.shape, mybir.dt.from_np(v.dtype), kind="ExternalInput").ap() for k, v in arrays.items()]
    args.append(nc.dram_tensor("out", (B, T, D), mybir.dt.float32, kind="ExternalOutput").ap())
    xattn_pair(nc, *args)
    r = run_bass_kernel_spmd(nc, [arrays], core_ids=[0])
    return r.results[0]["out"]
```

```python
import concourse.bass as bass
from concourse import mybir
from contextlib import ExitStack

B, T, D, K, H = 16, 512, 256, 64, 16
HD = D // H
P = 128
DC = D // P
TT = T // P
SHIFTS = 3
HPH = H // DC
EPS_RMS = 1.1920929e-07
EPS_DEN = 1e-06
LN_EPS = 1e-05
CT = B * K // P
RING = 4

C_ID, C_SEL, C_POS, C_EPS, C_END = 0, 128, 224, 227, 228


def xattn_pair(nc: bass.Bass, xT, ctx, ctxT, idx, vectors, wq0T, wk0T, wv0T, wo0T,
               wq1, wk1, wv1, wf1, bf1, ln_g, ln_b, consts, out):
    f32 = mybir.dt.float32
    f32r = mybir.dt.float32r
    i32 = mybir.dt.int32
    ALU = mybir.AluOpType
    ACT = mybir.ActivationFunctionType
    AX = mybir.AxisListType

    es = ExitStack()
    with es:
        def sb(name, shape, dt=f32):
            return es.enter_context(nc.sbuf_tensor(name, shape, dt))

        def sem(name):
            return es.enter_context(nc.semaphore(name))

        cst = sb("cst", [P, C_END])
        ident = cst[:, C_ID:C_ID + P]
        sum_sel = cst[:, C_SEL:C_SEL + 96].rearrange("p (g c) -> p g c", g=3)
        pos = [cst[:, C_POS + s:C_POS + s + 1] for s in range(SHIFTS)]
        den_eps = cst[:, C_EPS:C_EPS + 1]
        vec = sb("vec", [P, 5, DC])
        bf_row = sb("bf_row", [P, D])
        lng_row = sb("lng_row", [P, D])
        lnb_row = sb("lnb_row", [P, D])
        minus_half = sb("minus_half", [P, CT])
        zeros = sb("zeros", [P, 2 * D])
        x_ring = sb("x_ring", [P, RING, DC, T])
        idx_ring = sb("idx_ring", [P, RING, T], i32)
        kv0 = sb("kv0", [P, B, 2, D])
        vfd = sb("vfd", [P, B, D])
        k1T = sb("k1T", [P, DC, B * K + K])

        w_hi = {n: sb("wh_" + n, [P, DC, D], f32r) for n in ("q0", "o0", "q1")}
        w_lo = {n: sb("wl_" + n, [P, DC, D], f32r) for n in ("q0", "o0", "q1")}

        kv = sb("kv", [P, 2, D], f32r)
        onehot = sb("onehot", [P, SHIFTS, T], f32r)
        vf_hi = sb("vf_hi", [P, D], f32r)
        vf_lo = sb("vf_lo", [P, D], f32r)
        x_hi = sb("x_hi", [P, DC, T], f32r)
        x_lo = sb("x_lo", [P, DC, T], f32r)
        qkp = sb("qkp", [P, 2 * SHIFTS, DC * T])
        qk = qkp[:, 0:SHIFTS, :].rearrange("p s (c t) -> p s c t", c=DC)
        att = qkp[:, SHIFTS:2 * SHIFTS, :].rearrange("p s (j d) -> p s j d", j=TT)
        s_sb = sb("s_sb", [P, T])
        w = sb("w", [P, SHIFTS, TT, H])
        den = sb("den", [P, TT, H])
        dcl = sb("dcl", [P, TT, H])
        rden = sb("rden", [P, TT, H])
        wn = sb("wn", [P, SHIFTS, TT, H])
        o_hi = sb("o_hi", [P, DC, T], f32r)
        o_lo = sb("o_lo", [P, DC, T], f32r)
        xp_hi = sb("xp_hi", [P, DC, T], f32r)
        xp_lo = sb("xp_lo", [P, DC, T], f32r)
        smax = sb("smax", [P, TT])
        sdiff = sb("sdiff", [P, TT, K])
        ex = sb("ex", [P, TT, K])
        ssum = sb("ssum", [P, TT])
        rsum = sb("rsum", [P, TT])
        enf = sb("enf", [P, TT, K])
        en = sb("en", [P, TT, 2, K], f32r)
        eT = sb("eT", [P, T], f32r)
        stats = sb("stats", [P, TT, 6])
        mean_gap, nmean2, m2_sum, gap_sq, var = (sb(n, [P, TT]) for n in ("mean_gap", "nmean2", "m2_sum", "gap_sq", "var"))
        rstd = sb("rstd", [P, TT])
        nmean = sb("nmean", [P, TT])
        nbias = sb("nbias", [P, TT])
        bufs = sb("bufs", [P, 8, DC * T])
        xsq, q0, xpT, q1T = (bufs[:, n, :].rearrange("p (c t) -> p c t", c=DC) for n in (0, 3, 4, 5))
        zn, zo = (bufs[:, n, :].rearrange("p (j d) -> p j d", j=TT) for n in (6, 7))

        def rows(t):
            return t.rearrange("p a b -> p (a b)").rearrange("p (t d) -> p t d", d=D)

        ctx_sb = rows(qkp[:, 0:2, :])
        kn = rows(qkp[:, 2:4, :])
        knT = bufs[:, 0:2, :]
        kv_hi = [[rows(t[:, :, :]) for t in pair] for pair in ((xp_hi, xp_lo), (o_hi, o_lo))]
        kv_lo = [[rows(qkp[:, n:n + 1, :]) for n in pair] for pair in ((0, 4), (1, 5))]
        v1T = bufs[:, 4:6, :]
        ctxT_sb = bufs[:, 6:8, :]
        vfn = rows(bufs[:, 6:8, :])
        raw = {n: vfd[:, 2 * i:2 * i + 2, :] for i, n in enumerate(("k0", "v0", "k1", "v1", "f1", "q0", "o0", "q1"))}
        csq = x_ring[:, RING - 1, 0, 0:D]
        cms = sb("cms", [P, CT])
        cmean = sb("cmean", [P, CT])
        crs = sb("crs", [P, CT])

        ps = es.enter_context(nc.psum_tensor("ps", [P, 8, 512], f32))

        consts_in, ctx_in, wk1_in, wv1_in, w0_in, w1_in, x_in, idx_in = map(sem, (
            "consts_in", "ctx_in", "wk1_in", "wv1_in", "w0_in", "w1_in", "x_in", "idx_in"))
        ctxT_in = [sem("ctxT_in0"), sem("ctxT_in1")]
        folded, weights_hi, weights_ready, cms_done, cmean_done, crs_done, kn_done, knT_mm, knT_cp, half_set, k1_padded = map(sem, (
            "folded", "weights_hi", "weights_ready", "cms_done", "cmean_done", "crs_done", "kn_done", "knT_mm", "knT_cp",
            "half_set", "k1_padded"))
        kv0_in = [sem(f"kv0_in_{t}") for t in range(2)]
        prep_mm, prep_act, prep_dve, kvh_cp, vf_mm, vf_copied, vfd_in = map(sem, (
            "prep_mm", "prep_act", "prep_dve", "kvh_cp", "vf_mm", "vf_copied", "vfd_in"))
        kv_ready, vfh_ready, vf_ready = map(sem, ("kv_ready", "vfh_ready", "vf_ready"))
        onehot_ready, xsq_ready, xh_ready, xl_ready = map(sem, ("onehot_ready", "xsq_ready", "xh_ready", "xl_ready"))
        q0_mm, q0_cp, kg_mm, qk_ready, s_mm, s_cp, sT_mm, w_ready = map(sem, (
            "q0_mm", "q0_cp", "kg_mm", "qk_ready", "s_mm", "s_cp", "sT_mm", "w_ready"))
        den_ready, dcl_ready, rden_ready, wn_ready, vg_mm, att_ready, o_mm, oh_ready, ol_ready = map(sem, (
            "den_ready", "dcl_ready", "rden_ready", "wn_ready", "vg_mm", "att_ready", "o_mm", "oh_ready", "ol_ready"))
        xp_mm, xp_ready, xph_ready, xpl_ready, q1_mm, q1_ready, sc_mm = map(sem, (
            "xp_mm", "xp_ready", "xph_ready", "xpl_ready", "q1_mm", "q1_ready", "sc_mm"))
        smax_ready, sdiff_ready, ex_ready, ssum_ready, rsum_ready, enf_ready, enh_ready, en_ready = map(sem, (
            "smax_ready", "sdiff_ready", "ex_ready", "ssum_ready", "rsum_ready", "enf_ready", "enh_ready", "en_ready"))
        eT_mm, eT_ready, z_mm = map(sem, ("eT_mm", "eT_ready", "z_mm"))
        stats_ready, parts_ready, gap_ready, var_ready, rstd_ready, nmean_ready, nbias_ready = map(sem, (
            "stats_ready", "parts_ready", "gap_ready", "var_ready", "rstd_ready", "nmean_ready", "nbias_ready"))
        zn_ready, zg_ready, zo_ready, out_done, last_zg, last_zo, last_out_done = map(sem, (
            "zn_ready", "zg_ready", "zo_ready", "out_done", "last_zg", "last_zo", "last_out_done"))

        block = es.enter_context(nc.Block())

        FIRST_STEADY, LAST_STEADY = 2, B - 1

        def steps(engine, step):
            step(0, None, None)
            step(1, 0, None)
            with engine.Fori(FIRST_STEADY, LAST_STEADY) as i:
                step(i, i - 1, i - 2)
            step(B - 1, B - 2, B - 3, last=True)
            step(None, B - 1, B - 2)
            step(None, None, B - 1)

        def steps_turned(engine, head, tail):
            head(0, None, None)
            tail(0, None)
            head(1, 0, None)
            tail(1, 0)
            head(FIRST_STEADY, FIRST_STEADY - 1, FIRST_STEADY - 2)
            with engine.Fori(FIRST_STEADY, LAST_STEADY) as i:
                tail(i, i - 1)
                head(i + 1, i, i - 1)
            tail(B - 1, B - 2, last=True)
            head(None, B - 1, B - 2)
            tail(None, B - 1)
            head(None, None, B - 1)

        def first(n):
            return isinstance(n, int) and n == 0

        def is_last(n):
            return isinstance(n, int) and n == B - 1

        def f32_view(t):
            return t.bitcast(f32)

        RESULTS = ["act"] * 4 + ["act"] * 4 + ["dve"] * (2 * CT)
        K1, V1, KV = 0, 4, 8

        def final_bank(t):
            return 6 + t % 2 if t < 6 else t - 4

        def copied_until(n, engine):
            return sum(e == engine for e in RESULTS[:n + 1])

        @block.sync
        def _(sp):
            def weight(name, src, done):
                sp.dma_start(raw[name], src.rearrange("(c p) e -> p c e", p=P)).then_inc(done, 16)

            def load(i):
                sp.dma_start(x_ring[:, i % RING, :, :], xT[i].rearrange("(c p) t -> p c t", p=P)).then_inc(x_in, 16)
                sp.dma_start(idx_ring[:, i % RING, :], idx[i].partition_broadcast(P)).then_inc(idx_in, 16)

            weight("k1", wk1, wk1_in)
            for n in range(2):
                rows = slice(n * 512, (n + 1) * 512)
                sp.dma_start(ctxT_sb[:, :, rows], ctxT[:, rows].rearrange("(c p) n -> p c n", p=P)).then_inc(ctxT_in[n], 16)
                if n == 0:
                    sp.dma_start(vec[:, :, :], vectors).then_inc(consts_in, 16)
                    sp.dma_start(ctx_sb, ctx.rearrange("(t p) d -> p t d", p=P)).then_inc(ctx_in, 16)
            weight("v1", wv1, wv1_in)
            sp.dma_start(cst[:, :], consts).then_inc(consts_in, 16)
            weight("k0", wk0T, w0_in)
            weight("v0", wv0T, w0_in)
            weight("q0", wq0T, w0_in)
            load(0)
            weight("o0", wo0T, w1_in)
            weight("q1", wq1, w1_in)
            weight("f1", wf1, w1_in)
            for t, v in ((bf_row, bf1), (lng_row, ln_g), (lnb_row, ln_b)):
                sp.dma_start(t[:, :], v.partition_broadcast(P)).then_inc(w1_in, 16)
            sp.wait_ge(x_in, 16)
            sp.wait_ge(idx_in, 16)
            load(1)
            for t in range(2):
                sp.wait_ge(prep_dve, 2 * 4 * (t + 1))
                for odd in range(2):
                    half = slice(odd * K, (odd + 1) * K)
                    for m in range(2):
                        sp.dma_start(kv0[0:K, 8 * t + odd:8 * t + 8:2, m, :], f32_view(kv_hi[m][t][half, :, :])).then_inc(kv0_in[t], 16)
                        sp.dma_start(kv0[K:P, 8 * t + odd:8 * t + 8:2, m, :], kv_lo[m][t][half, :, :]).then_inc(kv0_in[t], 16)
            for i in range(2, RING):
                sp.wait_ge(x_in, 16 * i)
                sp.wait_ge(idx_in, 16 * i)
                load(i)
            sp.wait_ge(vf_copied, CT)
            sp.wait_ge(weights_ready, 3)
            for half in range(2):
                for odd in range(2):
                    sp.dma_start(vfd[half * K:(half + 1) * K, odd::2, :], vfn[odd * K:(odd + 1) * K, :, :]).then_inc(vfd_in, 16)
            with sp.Fori(1, B - RING + 1) as read:
                sp.wait_ge(xp_ready, 2 * read)
                sp.wait_ge(onehot_ready, read)
                sp.wait_ge(x_in, 16 * read + 16 * (RING - 1))
                sp.wait_ge(idx_in, 16 * read + 16 * (RING - 1))
                load(read + (RING - 1))
            for h in range(2):
                sp.wait_ge(last_zo, h + 1)
                sp.dma_start(out[B - 1, 2 * h * P:(2 * h + 2) * P, :].rearrange("(j p) d -> p j d", p=P),
                             zo[:, 2 * h:2 * h + 2, :]).then_inc(last_out_done, 16)
            sp.wait_ge(last_out_done, 16 * 2)

        @block.gpsimd
        def _(pool):
            G = nc.gpsimd
            G.memset(minus_half[:, :], -0.5).then_inc(half_set, 1)
            G.memset(zeros[:, :], 0.0).then_inc(half_set, 1)
            G.memset(k1T[:, :, B * K:], 0.0).then_inc(k1_padded, 1)
            pool.wait_ge(cms_done, CT)
            G.tensor_scalar(cmean[:, :], cms[:, :], 1.0 / D, EPS_RMS, ALU.mult, ALU.add).then_inc(cmean_done, 1)
            pool.wait_ge(cmean_done, 1)
            pool.wait_ge(half_set, 2)
            G.tensor_tensor(crs[:, :], cmean[:, :], minus_half[:, :], ALU.pow).then_inc(crs_done, 1)

            def take_kv(f):
                G.tensor_tensor(kv[:, :, :].rearrange("p m d -> p (m d)"), kv0[:, f, :, :].rearrange("p m d -> p (m d)"),
                                zeros[:, :], ALU.add).then_inc(kv_ready, 1)

            def split_x_lo(f):
                pool.wait_ge(xh_ready, 2 * f + 2)
                G.tensor_tensor(x_lo[:, :, :], x_ring[:, f % RING, :, :], f32_view(x_hi[:, :, :]), ALU.subtract).then_inc(xl_ready, 2)

            pool.wait_ge(consts_in, 16 * 2)
            split_x_lo(0)
            pool.wait_ge(kv0_in[0], 16 * 8)
            take_kv(0)

            def step(f, b, n, last=False):
                if f is not None and not last:
                    split_x_lo(f + 1)
                if n is not None:
                    pool.wait_ge(var_ready, n + 1)
                    G.tensor_tensor(rstd[:, :], var[:, :], minus_half[:, 0:TT], ALU.pow).then_inc(rstd_ready, 1)
                    pool.wait_ge(rstd_ready, n + 1)
                    pool.wait_ge(nmean_ready, n + 1)
                    G.tensor_tensor(nbias[:, :], nmean[:, :], rstd[:, :], ALU.mult).then_inc(nbias_ready, 1)
                if b is not None:
                    if n is not None:
                        pool.wait_ge(z_mm, n + 1)
                    else:
                        pool.wait_ge(vfd_in, 16 * 4)
                    G.tensor_tensor(vf_hi[:, :], vfd[:, b, :], zeros[:, 0:D], ALU.add).then_inc(vfh_ready, 1)
                if n is not None and not is_last(n):
                    pool.wait_ge(zn_ready, 2 * n + 2)
                    if not first(n):
                        pool.wait_ge(out_done, 16 * n)
                    G.tensor_tensor(zo, zn, lng_row[:, :].unsqueeze(1).broadcast_to([P, TT, D]), ALU.mult).then_inc(zg_ready, 1)
                    pool.wait_ge(zg_ready, n + 1)
                    G.tensor_tensor(zo, zo, lnb_row[:, :].unsqueeze(1).broadcast_to([P, TT, D]), ALU.add).then_inc(zo_ready, 1)
                    pool.wait_ge(zo_ready, n + 1)
                    pool.dma_start(out[n].rearrange("(j p) d -> p j d", p=P), zo).then_inc(out_done, 16)
                if f is not None and not last:
                    if first(f):
                        pool.wait_ge(kv0_in[1], 16 * 8)
                    pool.wait_ge(vg_mm, 3 * f + 3)
                    take_kv(f + 1)

            steps(pool, step)
            pool.wait_ge(out_done, 16 * (B - 1))

        @block.tensor
        def _(pe):
            mm = nc.tensor.matmul

            def result(n, parts):
                if n >= 4:
                    owner = RESULTS[n - 4]
                    pe.wait_ge(prep_act if owner == "act" else prep_dve, copied_until(n - 4, owner))
                for i, (stationary, moving, cols) in enumerate(parts):
                    last = mm(ps[:, 4 + n % 4, 0:cols], stationary, moving, start=(i == 0), stop=(i == len(parts) - 1))
                last.then_inc(prep_mm, 1)

            def transposed(n0, name, src):
                for n in range(2):
                    if name == "k1":
                        pe.wait_ge(ctxT_in[n], 16)
                    for e in range(DC):
                        result(n0 + 2 * n + e, [(raw[name][:, c, e * P:(e + 1) * P], src[:, c, n * 512:(n + 1) * 512], 512)
                                                for c in range(DC)])

            pe.wait_ge(wk1_in, 16)
            transposed(K1, "k1", ctxT_sb)
            pe.wait_ge(wv1_in, 16)
            transposed(V1, "v1", ctxT_sb)
            pe.wait_ge(consts_in, 16 * 2)
            for t in range(CT):
                pe.wait_ge(kn_done, t + 1)
                if t >= 4:
                    pe.wait_ge(knT_cp, t - 3)
                for c in range(DC):
                    last = nc.tensor.transpose(ps[:, t % 4, c * P:(c + 1) * P], kn[:, t, c * P:(c + 1) * P], ident)
                last.then_inc(knT_mm, 1)
            pe.wait_ge(knT_cp, CT)
            pe.wait_ge(folded, 3)
            for t in range(CT):
                for m, name in enumerate(("k0", "v0")):
                    result(KV + 2 * t + m, [(knT[:, c, t * P:(t + 1) * P], raw[name][:, c, :], D) for c in range(DC)])
            pe.wait_ge(weights_ready, 3)
            pe.wait_ge(k1_padded, 1)

            def final_values(tiles):
                for t in tiles:
                    if t == 0:
                        pe.wait_ge(w1_in, 16 * 6)
                        pe.wait_ge(prep_act, copied_until(KV - 1, "act"))
                    if t < 2:
                        pe.wait_ge(prep_dve, 2 * CT)
                    elif t < 6:
                        pe.wait_ge(vf_copied, t - 1)
                    for c in range(DC):
                        last = mm(ps[:, final_bank(t), 0:D], v1T[:, c, t * P:(t + 1) * P], raw["f1"][:, c, :],
                                  start=(c == 0), stop=(c == DC - 1))
                    last.then_inc(vf_mm, 1)

            def product(o, hi, lo, m_hi, m_lo, start, stop, done=None):
                mm(o, hi, m_hi, start=start, stop=False)
                mm(o, lo, m_hi, start=False, stop=False)
                last = mm(o, hi, m_lo, start=False, stop=stop)
                if stop and done is not None:
                    last.then_inc(done, 1)
                return last

            def weight(name, c, e):
                return (t[name][:, c, e * P:(e + 1) * P] for t in (w_hi, w_lo))

            def picked_keys(f, s, bank0):
                for g in range(DC):
                    i = mm(ps[:, bank0 + g, :], kv[:, 0, g * P:(g + 1) * P], onehot[:, s, :], start=True, stop=True)
                i.then_inc(kg_mm, 1)

            def picked_values(f, s, bank0):
                for j in range(TT):
                    i = mm(ps[:, bank0 + j // 2, (j % 2) * D:(j % 2 + 1) * D], onehot[:, s, j * P:(j + 1) * P], kv[:, 1, :],
                           start=True, stop=True)
                i.then_inc(vg_mm, 1)

            def first_keys(f):
                pe.wait_ge(kv_ready, f + 1)
                pe.wait_ge(onehot_ready, f + 1)
                picked_keys(f, 0, 4)

            def queries0(e):
                for c in range(DC):
                    product(ps[:, e, :], *weight("q0", c, e), x_hi[:, c, :], x_lo[:, c, :], c == 0, c == DC - 1, q0_mm)

            def turn(f, s):
                pe.wait_ge(att_ready, 3 * f + s + 1)
                for g in range(DC):
                    for j in range(TT):
                        i = mm(ps[:, g, j * P:(j + 1) * P], att[:, s, j, g * P:(g + 1) * P], ident,
                               is_transpose=True, start=(s == 0 and j == 0), stop=(s == SHIFTS - 1), skip_group_check=True)
                    if s == SHIFTS - 1:
                        i.then_inc(o_mm, 1)

            pe.wait_ge(xh_ready, 2)
            pe.wait_ge(xl_ready, 2)
            queries0(0)
            queries0(1)
            final_values(range(0, 2))
            first_keys(0)

            def step(f, b, n, last=False):
                if b is not None:
                    pe.wait_ge(oh_ready, 2 * b + 2)
                    pe.wait_ge(ol_ready, 2 * b + 2)
                if f is not None:
                    pe.wait_ge(q0_cp, 2 * f + 2)
                    picked_keys(f, 1, 0)
                    if first(f):
                        final_values(range(2, 4))
                if n is not None:
                    pe.wait_ge(eT_ready, n + 1)
                    pe.wait_ge(vf_ready, n + 1)
                    for j in range(TT):
                        at = (j % 2) * D
                        for part in (vf_hi, vf_lo):
                            i = mm(ps[:, 6 + j // 2, at:at + D], eT[:, j * P:(j + 1) * P], part[:, :],
                                   start=False, stop=(part is vf_lo), skip_group_check=True)
                    i.then_inc(z_mm, 1)
                if f is not None:
                    pe.wait_ge(qk_ready, 3 * f + 1)
                    picked_keys(f, 2, 4)
                if b is not None:
                    if first(b):
                        pe.wait_ge(vf_copied, CT)
                    for e in range(DC):
                        for c in range(DC):
                            product(ps[:, 2 + e, :], *weight("o0", c, e), o_hi[:, c, :], o_lo[:, c, :], c == 0, c == DC - 1, xp_mm)
                if f is not None:
                    if not last:
                        pe.wait_ge(xh_ready, 2 * f + 4)
                        pe.wait_ge(xl_ready, 2 * f + 4)
                        pe.wait_ge(qk_ready, 3 * f + 2)
                        queries0(0)
                    pe.wait_ge(qk_ready, 3 * f + 3)
                    pe.wait_ge(xsq_ready, f + 1)
                    for g in range(DC):
                        for s in range(SHIFTS + 1):
                            i = mm(ps[32 * s:32 * s + 32, 4, :], sum_sel[:, g if s < SHIFTS else 2, :],
                                   qk[:, s, g, :] if s < SHIFTS else xsq[:, g, :], start=(g == 0), stop=(g == DC - 1))
                    i.then_inc(s_mm, 1)

                def queries1(e):
                    for c in range(DC):
                        product(ps[:, 2 + e, :], *weight("q1", c, e), xp_hi[:, c, :], xp_lo[:, c, :], c == 0, c == DC - 1, q1_mm)

                if f is not None:
                    if not last:
                        queries0(1)
                    pe.wait_ge(s_cp, f + 1)
                    for j in range(TT):
                        i = nc.tensor.transpose(ps[:, 5, j * P:(j + 1) * P], s_sb[:, j * P:(j + 1) * P], ident)
                    i.then_inc(sT_mm, 1)
                    if first(f):
                        final_values(range(4, 6))
                if b is not None:
                    pe.wait_ge(xph_ready, 2 * b + 2)
                    pe.wait_ge(xpl_ready, 2 * b + 2)
                    queries1(0)
                    if f is None:
                        pe.wait_ge(zn_ready, 2 * b)
                if f is not None:
                    pe.wait_ge(w_ready, f + 1)
                    pe.wait_ge(dcl_ready, f + 1)
                    picked_values(f, 0, 4)
                    if first(f):
                        final_values(range(6, 7))
                        pe.wait_ge(vf_copied, 6)
                    if b is not None and not first(b):
                        pe.wait_ge(zn_ready, 2 * b)
                    picked_values(f, 1, 6)
                    if first(f):
                        final_values(range(7, CT))
                if b is not None:
                    queries1(1)
                if f is not None:
                    pe.wait_ge(att_ready, 3 * f + 1)
                    picked_values(f, 2, 4)
                if b is not None:
                    pe.wait_ge(q1_ready, b + 1)
                    for j in range(TT):
                        for c in range(DC):
                            i = mm(ps[:, 3, j * P:(j + 1) * P], q1T[:, c, j * P:(j + 1) * P],
                                   k1T[:, c, bass.ds(b * K, 2 * K)], start=(c == 0), stop=(c == DC - 1))
                    i.then_inc(sc_mm, 1)

                def back(j):
                    for c in range(DC):
                        at = (j % 2) * D + c * P
                        mm(ps[:, 6 + j // 2, at:at + P], xpT[:, c, j * P:(j + 1) * P], ident,
                           is_transpose=True, start=(at == 0), stop=False, skip_group_check=True)

                if f is not None:
                    if not last:
                        pe.wait_ge(q0_cp, 2 * f + 4)
                    for s in range(SHIFTS):
                        turn(f, s)
                if b is not None:
                    for j in range(TT):
                        back(j)
                    pe.wait_ge(en_ready, b + 1)
                    for j in range(TT):
                        i = nc.tensor.transpose(ps[:, 3, j * P:(j + 1) * P],
                                                f32_view(en[:, j, :, :]).rearrange("p a k -> p (a k)"), ident)
                    i.then_inc(eT_mm, 1)
                if f is not None and not last:
                    first_keys(f + 1)

            steps(pe, step)

        @block.scalar
        def _(act):
            A = nc.scalar.activation
            act.wait_ge(consts_in, 16 * 2)
            act.wait_ge(ctx_in, 16)
            for t in range(CT):
                if t:
                    act.wait_ge(cms_done, t)
                A(csq, ctx_sb[:, t, :], ACT.Square, accum_out=cms[:, t:t + 1]).then_inc(cms_done, 1)

            def copy_out(n, dst, cols, func, **kw):
                act.wait_ge(prep_mm, n + 1)
                return A(dst, ps[:, 4 + n % 4, 0:cols], func, **kw)

            for n0, dst, bias in ((K1, k1T, 3), (V1, v1T, 4)):
                for h in range(2):
                    for e in range(DC):
                        copy_out(n0 + 2 * h + e, dst[:, e, h * 512:(h + 1) * 512], 512, ACT.Gelu,
                                 bias=vec[:, bias, e:e + 1]).then_inc(prep_act, 1)
            for t in range(CT):
                act.wait_ge(knT_mm, t + 1)
                A(knT[:, :, t * P:(t + 1) * P], ps[:, t % 4, 0:D].rearrange("p (c n) -> p c n", c=DC), ACT.Copy).then_inc(knT_cp, 1)

            def split_x_hi(f):
                act.wait_ge(x_in, 16 * f + 16)
                if not first(f):
                    act.wait_ge(q0_mm, 2 * f)
                A(x_hi[:, :, :], x_ring[:, f % RING, :, :], ACT.Copy).then_inc(xh_ready, 2)

            split_x_hi(0)
            for t in range(CT):
                for m in range(2):
                    copy_out(KV + 2 * t + m, kv_hi[m][t // 4][:, t % 4, :], D, ACT.Copy).then_inc(kvh_cp, 1)

            def copy_q0(f, g):
                act.wait_ge(q0_mm, 2 * f + g + 1)
                A(q0[:, g, :], ps[:, g, :], ACT.Copy).then_inc(q0_cp, 1)

            copy_q0(0, 0)
            copy_q0(0, 1)

            def normalise(tiles):
                for j in tiles:
                    i = A(zn[:, j, :], ps[:, 6 + j // 2, (j % 2) * D:(j % 2 + 1) * D], ACT.Identity,
                          bias=nbias[:, j:j + 1], scale=rstd[:, j:j + 1])
                i.then_inc(zn_ready, 1)

            def step(f, b, n, last=False):
                if f is not None:
                    if not last:
                        split_x_hi(f + 1)
                    if not first(f):
                        act.wait_ge(s_mm, f)
                    A(xsq, x_ring[:, f % RING, :, :], ACT.Square).then_inc(xsq_ready, 1)

                def round_xp():
                    for g in range(DC):
                        act.wait_ge(xp_ready, 2 * b + g + 1)
                        A(xp_hi[:, g, :], xpT[:, g, :], ACT.Copy).then_inc(xph_ready, 1)

                if b is not None and f is None:
                    round_xp()
                if n is not None:
                    act.wait_ge(z_mm, n + 1)
                    act.wait_ge(nbias_ready, n + 1)
                    if not first(n):
                        act.wait_ge(zg_ready, n)
                    normalise(range(0, 2))
                if b is not None and f is not None:
                    round_xp()
                if f is not None:
                    act.wait_ge(s_mm, f + 1)
                    A(s_sb[:, :], ps[:, 4, :], ACT.Relu, bias=den_eps).then_inc(s_cp, 1)
                    if not last:
                        copy_q0(f + 1, 0)
                    act.wait_ge(sT_mm, f + 1)
                    A(w[:, :, :, :].rearrange("p s j h -> p j s h"),
                      ps[:, 5, :].rearrange("p (j s h) -> p j s h", j=TT, h=32)[:, :, 0:SHIFTS, 0:H], ACT.Square).then_inc(w_ready, 1)
                if n is not None:
                    normalise(range(2, TT))
                if b is not None:
                    for e in range(DC):
                        if e == 1 and f is not None and not last:
                            copy_q0(f + 1, 1)
                        act.wait_ge(q1_mm, 2 * b + e + 1)
                        i = A(q1T[:, e, :], ps[:, 2 + e, :], ACT.Gelu, bias=vec[:, 2, e:e + 1])
                    i.then_inc(q1_ready, 1)
                elif f is not None:
                    copy_q0(f + 1, 1)
                if b is not None:
                    act.wait_ge(sdiff_ready, b + 1)
                    A(ex[:, :, :], sdiff[:, :, :], ACT.Exp).then_inc(ex_ready, 1)
                if f is not None:
                    for g in range(DC):
                        act.wait_ge(o_mm, 2 * f + g + 1)
                        A(o_hi[:, g, :], ps[:, g, :], ACT.Copy).then_inc(oh_ready, 1)
                if b is not None:
                    act.wait_ge(eT_mm, b + 1)
                    A(eT[:, :], ps[:, 3, :], ACT.Copy).then_inc(eT_ready, 1)

            steps(act, step)

        @block.vector
        def _(dve):
            V = nc.vector
            dve.wait_ge(consts_in, 16 * 2)
            dve.wait_ge(w0_in, 16 * 3)
            for n, g in (("k0", 1), ("v0", 1), ("q0", 0)):
                for c in range(DC):
                    last = V.tensor_scalar(raw[n][:, c, :], raw[n][:, c, :], vec[:, g, c:c + 1], None, ALU.mult)
                last.then_inc(folded, 1)
            dve.wait_ge(crs_done, 1)
            for t in range(CT):
                V.tensor_scalar(kn[:, t, :], ctx_sb[:, t, :], crs[:, t:t + 1], None, ALU.mult).then_inc(kn_done, 1)
            dve.wait_ge(w1_in, 16 * 6)
            dve.wait_ge(folded, 3)
            for i, n in enumerate(("q0", "o0", "q1")):
                V.tensor_copy(w_hi[n][:, :, :], raw[n]).then_inc(weights_hi, 1)
                dve.wait_ge(weights_hi, i + 1)
                V.tensor_tensor(w_lo[n][:, :, :], raw[n], f32_view(w_hi[n][:, :, :]), ALU.subtract).then_inc(weights_ready, 1)
            for t in range(CT):
                for m in range(2):
                    dve.wait_ge(kvh_cp, 2 * t + m + 1)
                    V.tensor_tensor(kv_lo[m][t // 4][:, t % 4, :], ps[:, 4 + (KV + 2 * t + m) % 4, 0:D],
                                    f32_view(kv_hi[m][t // 4][:, t % 4, :]), ALU.subtract).then_inc(prep_dve, 1)

            def copy_final_values(tiles):
                for t in tiles:
                    dve.wait_ge(vf_mm, t + 1)
                    V.tensor_tensor(vfn[:, t, :], ps[:, final_bank(t), 0:D], bf_row[:, :], ALU.add).then_inc(vf_copied, 1)

            def build_onehot(f, shifts):
                dve.wait_ge(idx_in, 16 * f + 16)
                if not first(f):
                    dve.wait_ge(vg_mm, 3 * f)
                for s in shifts:
                    i = V.tensor_scalar(onehot[:, s, :], idx_ring[:, f % RING, :], pos[s], None, ALU.is_equal)
                if s == SHIFTS - 1:
                    i.then_inc(onehot_ready, 1)

            build_onehot(0, range(SHIFTS))

            def multiply_keys(f, s, bank0):
                if s == 0:
                    dve.wait_ge(q0_cp, 2 * f + 2)
                    if not first(f):
                        dve.wait_ge(s_mm, f)
                dve.wait_ge(kg_mm, 3 * f + s + 1)
                V.tensor_tensor(qk[:, s, :, :], ps[:, bank0:bank0 + 2, :], q0, ALU.mult).then_inc(qk_ready, 1)

            def head(f, b, n):
                if f is not None:
                    if first(f):
                        copy_final_values(range(0, 2))
                    multiply_keys(f, 0, 4)
                    multiply_keys(f, 1, 0)
                if n is not None:
                    dve.wait_ge(z_mm, n + 1)
                    for j in range(TT):
                        i = V.bn_stats(stats[:, j, :], ps[:, 6 + j // 2, (j % 2) * D:(j % 2 + 1) * D])
                    i.then_inc(stats_ready, 1)
                    dve.wait_ge(stats_ready, n + 1)
                    mean_e, m2_e, mean_o, m2_o = (stats[:, :, i] for i in (1, 2, 4, 5))
                    V.tensor_tensor(mean_gap[:, :], mean_e, mean_o, ALU.subtract)
                    V.scalar_tensor_tensor(nmean2[:, :], mean_e, -1.0, mean_o, ALU.mult, ALU.subtract)
                    V.scalar_tensor_tensor(m2_sum[:, :], m2_e, D * LN_EPS, m2_o, ALU.add, ALU.add).then_inc(parts_ready, 1)
                    dve.wait_ge(parts_ready, n + 1)
                    V.scalar_tensor_tensor(gap_sq[:, :], mean_gap[:, :], 0.25, mean_gap[:, :], ALU.mult, ALU.mult).then_inc(gap_ready, 1)
                    V.tensor_scalar(nmean[:, :], nmean2[:, :], 0.5, None, ALU.mult).then_inc(nmean_ready, 1)
                    dve.wait_ge(gap_ready, n + 1)
                    V.scalar_tensor_tensor(var[:, :], m2_sum[:, :], 1.0 / D, gap_sq[:, :], ALU.mult, ALU.add).then_inc(var_ready, 1)
                if f is not None:
                    multiply_keys(f, 2, 4)
                    if first(f):
                        copy_final_values(range(2, 4))
                if b is not None:
                    for g in range(DC):
                        dve.wait_ge(xp_mm, 2 * b + g + 1)
                        V.tensor_tensor(xpT[:, g, :], ps[:, 2 + g, :], x_ring[:, b % RING, g, :], ALU.add).then_inc(xp_ready, 1)
                    for g in range(DC):
                        dve.wait_ge(xph_ready, 2 * b + g + 1)
                        V.tensor_tensor(xp_lo[:, g, :], xpT[:, g, :], f32_view(xp_hi[:, g, :]), ALU.subtract).then_inc(xpl_ready, 1)
                    dve.wait_ge(vfh_ready, b + 1)
                    V.tensor_tensor(vf_lo[:, :], vfd[:, b, :], f32_view(vf_hi[:, :]), ALU.subtract).then_inc(vf_ready, 1)

            def tail(f, b, last=False):
                def attend(s, bank0):
                    dve.wait_ge(vg_mm, 3 * f + s + 1)
                    V.tensor_tensor(att[:, s, :, :].rearrange("p j (h d) -> p (j h) d", d=HD),
                                    ps[:, bank0:bank0 + 2, :].rearrange("p a (h d) -> p (a h) d", d=HD),
                                    wn[:, s, :, :].rearrange("p j h -> p (j h)").unsqueeze(2).broadcast_to([P, TT * H, HD]),
                                    ALU.mult).then_inc(att_ready, 1)

                sc = ps[:, 3, :].rearrange("p (j n) -> p j n", n=P)[:, :, 0:K]

                def per_row(t):
                    return t[:, :].unsqueeze(2).broadcast_to([P, TT, K])

                if f is not None:
                    dve.wait_ge(w_ready, f + 1)
                    V.tensor_reduce(den[:, :, :].rearrange("p j h -> p (j h)"), w[:, :, :, :].rearrange("p s j h -> p (j h) s"),
                                    AX.X, ALU.add).then_inc(den_ready, 1)
                    dve.wait_ge(den_ready, f + 1)
                    V.tensor_tensor(dcl[:, :, :], den[:, :, :],
                                    ps[:, 5, :].rearrange("p (j r) -> p j r", j=TT)[:, :, 96:97].broadcast_to([P, TT, H]),
                                    ALU.max).then_inc(dcl_ready, 1)
                    dve.wait_ge(dcl_ready, f + 1)
                    V.reciprocal(rden[:, :, :], dcl[:, :, :]).then_inc(rden_ready, 1)
                    dve.wait_ge(rden_ready, f + 1)
                    V.tensor_tensor(wn[:, :, :, :].rearrange("p s j h -> p s (j h)"), w[:, :, :, :].rearrange("p s j h -> p s (j h)"),
                                    rden[:, :, :].rearrange("p j h -> p (j h)").unsqueeze(1).broadcast_to([P, SHIFTS, TT * H]),
                                    ALU.mult).then_inc(wn_ready, 1)
                    if first(f):
                        copy_final_values(range(4, 6))
                        dve.wait_ge(kv0_in[1], 16 * 8)
                    dve.wait_ge(wn_ready, f + 1)
                    if not first(f):
                        dve.wait_ge(o_mm, 2 * f)
                    attend(0, 4)
                    attend(1, 6)
                    attend(2, 4)
                    if first(f):
                        copy_final_values(range(6, CT))
                    if not last:
                        build_onehot(f + 1, range(0, 2))
                if b is not None:
                    dve.wait_ge(sc_mm, b + 1)
                    V.tensor_reduce(smax[:, :], sc, AX.X, ALU.max).then_inc(smax_ready, 1)
                    dve.wait_ge(smax_ready, b + 1)
                    V.tensor_tensor(sdiff[:, :, :], sc, per_row(smax), ALU.subtract).then_inc(sdiff_ready, 1)
                if f is not None and not last:
                    build_onehot(f + 1, range(2, SHIFTS))
                if b is not None:
                    dve.wait_ge(ex_ready, b + 1)
                    V.tensor_reduce(ssum[:, :], ex[:, :, :], AX.X, ALU.add).then_inc(ssum_ready, 1)
                    dve.wait_ge(ssum_ready, b + 1)
                    V.reciprocal(rsum[:, :], ssum[:, :]).then_inc(rsum_ready, 1)
                    dve.wait_ge(rsum_ready, b + 1)
                    V.tensor_tensor(enf[:, :, :], ex[:, :, :], per_row(rsum), ALU.mult).then_inc(enf_ready, 1)
                    dve.wait_ge(enf_ready, b + 1)
                    V.tensor_copy(en[:, :, 0, :], enf[:, :, :]).then_inc(enh_ready, 1)
                    dve.wait_ge(enh_ready, b + 1)
                    V.tensor_tensor(en[:, :, 1, :], enf[:, :, :], f32_view(en[:, :, 0, :]), ALU.subtract).then_inc(en_ready, 1)
                if f is not None:
                    for g in range(DC):
                        dve.wait_ge(oh_ready, 2 * f + g + 1)
                        V.tensor_tensor(o_lo[:, g, :], ps[:, g, :], f32_view(o_hi[:, g, :]), ALU.subtract).then_inc(ol_ready, 1)

            steps_turned(dve, head, tail)
            dve.wait_ge(w1_in, 16 * 6)
            for h in range(2):
                pair = slice(2 * h, 2 * h + 2)
                dve.wait_ge(zn_ready, 2 * (B - 1) + h + 1)
                if h == 0:
                    dve.wait_ge(out_done, 16 * (B - 1))
                V.tensor_tensor(zo[:, pair, :], zn[:, pair, :], lng_row[:, :].unsqueeze(1).broadcast_to([P, 2, D]), ALU.mult).then_inc(last_zg, 1)
                dve.wait_ge(last_zg, h + 1)
                V.tensor_tensor(zo[:, pair, :], zo[:, pair, :], lnb_row[:, :].unsqueeze(1).broadcast_to([P, 2, D]), ALU.add).then_inc(last_zo, 1)


def shape_constants():
    import numpy as np
    c = np.zeros((P, C_END), np.float32)
    r = np.arange(P)
    c[r, C_ID + r] = 1.0
    for g in range(DC):
        c[r, C_SEL + 32 * g + HPH * g + r // HD] = 1.0
    c[:, C_SEL + 64] = 16.0 * EPS_DEN / D
    for s in range(SHIFTS):
        c[:, C_POS + s] = r % K - 1 + s
    c[96, C_EPS] = 16.0 * EPS_DEN * EPS_RMS
    return c


def kernel(**inputs):
    import numpy as np
    import concourse.bacc as bacc
    from concourse.bass_utils import run_bass_kernel_spmd

    a = {k: np.asarray(v) for k, v in inputs.items()}

    ctx = a["ctx_1024"].reshape(B * K, D)
    arrays = {
        "xT": a["x"].transpose(0, 2, 1), "ctx": ctx, "ctxT": ctx.T, "idx": a["itok_BxS_0_255"],
        "vectors": np.stack([a[n].reshape(DC, P).T for n in ("L0_xattn_gamma_q", "L0_xattn_gamma_kv", "L1_xattn_bq",
                                                             "L1_xattn_bk", "L1_xattn_bv")], axis=1),
        "wq0T": a["L0_xattn_Wq"].T, "wk0T": a["L0_xattn_Wk"].T, "wv0T": a["L0_xattn_Wv"].T, "wo0T": a["L0_xattn_Wo"].T,
        "wq1": a["L1_xattn_Wq"], "wk1": a["L1_xattn_Wk"], "wv1": a["L1_xattn_Wv"],
        "wf1": a["L1_xattn_Wf"], "bf1": a["L1_xattn_bf"],
        "ln_g": a["L1_xattn_ln_gamma"], "ln_b": a["L1_xattn_ln_beta"],
        "consts": shape_constants(),
    }
    arrays = {k: np.ascontiguousarray(v) for k, v in arrays.items()}
    nc = bacc.Bacc("TRN2", target_bir_lowering=False, num_devices=1)
    args = [nc.dram_tensor(k, v.shape, mybir.dt.from_np(v.dtype), kind="ExternalInput").ap() for k, v in arrays.items()]
    args.append(nc.dram_tensor("out", (B, T, D), mybir.dt.float32, kind="ExternalOutput").ap())
    xattn_pair(nc, *args)
    r = run_bass_kernel_spmd(nc, [arrays], core_ids=[0])
    return r.results[0]["out"]
```
